# Optimizing a Trainium2 kernel written in Bass

```python
import numpy as np
import jax
import jax.numpy as jnp

def _softmax(x, axis=-1):
    return jax.nn.softmax(x, axis=axis)

def _gelu(x):
    return jax.nn.gelu(x, approximate=True)

def _silu(x):
    return jax.nn.silu(x)

def _sigmoid(x):
    return jax.nn.sigmoid(x)

def _layernorm(x, axis=-1, eps=1e-05):
    m = jnp.mean(x, axis=axis, keepdims=True)
    v = jnp.var(x, axis=axis, keepdims=True)
    return (x - m) / jnp.sqrt(v + eps)

def _scatter_add(tgt, idx, src, axis=0):
    return tgt.at[idx].add(src)

def _segment_sum(src, seg, n):
    return jax.ops.segment_sum(src, seg, n)
kernel_name = 'mk_gnn_resnorm_d2_gnn_r64_5e73b3'

def setup_inputs(seed: int=0):
    np.random.seed(seed)
    _w = jnp.asarray

    def _rec_inputs():
        import jax
        import jax.numpy as jnp
        _gk = jax.random.key(seed)
        x = -0.0003929 + 0.9999 * jax.random.normal(jax.random.fold_in(_gk, 1), (100000, 256), jnp.float32)
        src = jax.random.randint(jax.random.fold_in(_gk, 2), (25000,), 0, 100000, jnp.int32)
        dst = jnp.minimum((100000 * jax.random.uniform(jax.random.fold_in(_gk, 3), (25000,)) ** 2.0).astype(jnp.int32), 99999)
        _o = jnp.argsort(dst, stable=True)
        src = src[_o]
        dst = dst[_o]
        edge_attr_16 = -0.000153872 + 1.00011 * jax.random.normal(jax.random.fold_in(_gk, 12), (25000, 16), jnp.float32)
        edge_attr_4 = 0.0007022 + 0.999661 * jax.random.normal(jax.random.fold_in(_gk, 13), (25000, 4), jnp.float32)
        edge_weight = 0.00540447 + 1.00226 * jax.random.normal(jax.random.fold_in(_gk, 15), (25000,), jnp.float32)
        return (x, src, dst, edge_attr_16, edge_attr_4, edge_weight)
    x, src, dst, edge_attr_16, edge_attr_4, edge_weight = _rec_inputs()

    def _L0_gnn_setup():
        import jax, jax.numpy as jnp
        import numpy as np
        from itertools import combinations
        NDIM = 256
        BATCH = 1024

        def _build_mat(rots, idx_i, idx_j, ndim):

            def step(mat, t):
                i, j, theta = t
                c = jnp.cos(theta)
                s = jnp.sin(theta)
                ri = mat[i]
                rj = mat[j]
                mat = mat.at[i].set(c * ri - s * rj)
                mat = mat.at[j].set(s * ri + c * rj)
                return (mat, None)
            mat0 = jnp.eye(ndim, dtype=rots.dtype)
            mat, _ = jax.lax.scan(step, mat0, (idx_i, idx_j, rots))
            return mat.T
        key = jax.random.key(seed)
        k1, k2 = jax.random.split(key)
        pairs = np.array(list(combinations(range(NDIM), 2)), dtype=np.int32)
        return {'x': jax.random.normal(k1, (BATCH, NDIM), dtype=jnp.float32), 'rots': jax.random.normal(k2, (pairs.shape[0],), dtype=jnp.float32), 'idx_i': jnp.asarray(pairs[:, 0]), 'idx_j': jnp.asarray(pairs[:, 1])}
    _L0_gnn_all = _L0_gnn_setup()
    _L0_gnn_in = {k: v for k, v in _L0_gnn_all.items() if k in ()}
    del _L0_gnn_all

    def _L1_gnn_setup():
        import jax, jax.numpy as jnp
        import numpy as np
        N, E, C, R, HID = (50000, 500000, 64, 16, 64)
        key = jax.random.key(seed)
        ks = jax.random.split(key, 24)
        g = lambda k, shape, s=1.0: jax.random.normal(k, shape, dtype=jnp.float32) * s
        cs = C ** (-0.5)
        inp = {'h': g(ks[0], (N, 4 * C)), 'edge_index': jax.random.randint(ks[1], (2, E), 0, N), 'edge_sh': g(ks[2], (E, 4)), 'edge_rbf': g(ks[3], (E, R)), 'W_up0': g(ks[4], (C, C), cs), 'W_up1': g(ks[5], (C, C), cs), 'M1': g(ks[6], (R, HID), R ** (-0.5)), 'M2': g(ks[7], (HID, HID), HID ** (-0.5)), 'M3': g(ks[8], (HID, HID), HID ** (-0.5)), 'M4': g(ks[9], (HID, 4 * C), HID ** (-0.5)), 'W_lin0': g(ks[10], (C, C), cs), 'W_lin1': g(ks[11], (C, C), cs), 'Wsc0': g(ks[12], (C, C), cs), 'Wsc1': g(ks[13], (C, C), cs), 'Wc0': g(ks[14], (C, 5)), 'Wc1': g(ks[15], (C, 4)), 'WB0': g(ks[16], (C, C), cs), 'WB1': g(ks[17], (C, C), cs), 'gamma0': jnp.ones((C,), jnp.float32), 'beta0': jnp.zeros((C,), jnp.float32), 'gamma1': jnp.ones((C,), jnp.float32)}
        return inp
    _L1_gnn_all = _L1_gnn_setup()
    _L1_gnn_in = {k: v for k, v in _L1_gnn_all.items() if k in ('W_up0', 'W_up1', 'M1', 'M2', 'M3', 'M4', 'W_lin0', 'W_lin1', 'Wsc0', 'Wsc1', 'Wc0', 'Wc1', 'WB0', 'WB1', 'gamma0', 'beta0', 'gamma1')}
    del _L1_gnn_all
    return {'x': x, 'src': src, 'dst': dst, 'edge_attr_16': edge_attr_16, 'edge_attr_4': edge_attr_4, 'edge_weight': edge_weight, 'L1_gnn_W_up0': _L1_gnn_in['W_up0'], 'L1_gnn_W_up1': _L1_gnn_in['W_up1'], 'L1_gnn_M1': _L1_gnn_in['M1'], 'L1_gnn_M2': _L1_gnn_in['M2'], 'L1_gnn_M3': _L1_gnn_in['M3'], 'L1_gnn_M4': _L1_gnn_in['M4'], 'L1_gnn_W_lin0': _L1_gnn_in['W_lin0'], 'L1_gnn_W_lin1': _L1_gnn_in['W_lin1'], 'L1_gnn_Wsc0': _L1_gnn_in['Wsc0'], 'L1_gnn_Wsc1': _L1_gnn_in['Wsc1'], 'L1_gnn_Wc0': _L1_gnn_in['Wc0'], 'L1_gnn_Wc1': _L1_gnn_in['Wc1'], 'L1_gnn_WB0': _L1_gnn_in['WB0'], 'L1_gnn_WB1': _L1_gnn_in['WB1'], 'L1_gnn_gamma0': _L1_gnn_in['gamma0'], 'L1_gnn_beta0': _L1_gnn_in['beta0'], 'L1_gnn_gamma1': _L1_gnn_in['gamma1']}

def reference(x, src, dst, edge_attr_16, edge_attr_4, edge_weight, L1_gnn_W_up0, L1_gnn_W_up1, L1_gnn_M1, L1_gnn_M2, L1_gnn_M3, L1_gnn_M4, L1_gnn_W_lin0, L1_gnn_W_lin1, L1_gnn_Wsc0, L1_gnn_Wsc1, L1_gnn_Wc0, L1_gnn_Wc1, L1_gnn_WB0, L1_gnn_WB1, L1_gnn_gamma0, L1_gnn_beta0, L1_gnn_gamma1):
    import jax
    import jax.numpy as jnp

    def _L0_gnn_ref(x, rots, idx_i, idx_j):
        import jax, jax.numpy as jnp
        import numpy as np
        from itertools import combinations
        NDIM = 256
        BATCH = 1024

        def _build_mat(rots, idx_i, idx_j, ndim):

            def step(mat, t):
                i, j, theta = t
                c = jnp.cos(theta)
                s = jnp.sin(theta)
                ri = mat[i]
                rj = mat[j]
                mat = mat.at[i].set(c * ri - s * rj)
                mat = mat.at[j].set(s * ri + c * rj)
                return (mat, None)
            mat0 = jnp.eye(ndim, dtype=rots.dtype)
            mat, _ = jax.lax.scan(step, mat0, (idx_i, idx_j, rots))
            return mat.T
        m = _build_mat(rots, idx_i, idx_j, x.shape[-1])
        return x @ m

    def _L1_gnn_ref(h, edge_index, edge_sh, edge_rbf, W_up0, W_up1, M1, M2, M3, M4, W_lin0, W_lin1, Wsc0, Wsc1, Wc0, Wc1, WB0, WB1, gamma0, beta0, gamma1):
        import jax, jax.numpy as jnp
        import numpy as np
        N, E, C, R, HID = (50000, 500000, 64, 16, 64)
        n = h.shape[0]
        h0 = h[:, :C]
        h1 = h[:, C:].reshape(n, C, 3)
        up0 = h0 @ W_up0
        up1 = jnp.einsum('ncx,cd->ndx', h1, W_up1)
        r = jax.nn.silu(edge_rbf @ M1)
        r = jax.nn.silu(r @ M2)
        r = jax.nn.silu(r @ M3)
        tpw = (r @ M4).reshape(-1, 4, C)
        snd, rcv = (edge_index[0], edge_index[1])
        x0 = up0[snd]
        x1 = up1[snd]
        sh0 = edge_sh[:, 0]
        sh1 = edge_sh[:, 1:]
        inv3 = 1.0 / jnp.sqrt(jnp.float32(3.0))
        m0e = tpw[:, 0] * x0 * sh0[:, None] + tpw[:, 3] * jnp.einsum('ecx,ex->ec', x1, sh1) * inv3
        m1e = tpw[:, 1][:, :, None] * x0[:, :, None] * sh1[:, None, :] + tpw[:, 2][:, :, None] * x1 * sh0[:, None, None]
        msg0 = jax.ops.segment_sum(m0e, rcv, num_segments=n)
        msg1 = jax.ops.segment_sum(m1e, rcv, num_segments=n)
        A0 = msg0 @ W_lin0
        A1 = jnp.einsum('ncx,cd->ndx', msg1, W_lin1)
        sc0 = h0 @ Wsc0
        sc1 = jnp.einsum('ncx,cd->ndx', h1, Wsc1)
        vv = jnp.sum(A1 * A1, -1)
        B0 = Wc0[:, 0] * A0 + Wc0[:, 1] * A0 * A0 + Wc0[:, 2] * vv + Wc0[:, 3] * A0 ** 3 + Wc0[:, 4] * A0 * vv
        B1 = (Wc1[:, 0] + Wc1[:, 1] * A0 + Wc1[:, 2] * A0 * A0 + Wc1[:, 3] * vv)[..., None] * A1
        o0 = B0 @ WB0 + sc0
        o1 = jnp.einsum('ncx,cd->ndx', B1, WB1) + sc1
        eps = jnp.float32(1e-05)
        mu = jnp.mean(o0, 0)
        xc = o0 - mu
        var = jnp.mean(xc * xc, 0)
        n0 = xc * jax.lax.rsqrt(var + eps) * gamma0 + beta0
        nrm1 = jnp.mean(jnp.sum(o1 * o1, -1) / 3.0, 0)
        n1 = o1 * (jax.lax.rsqrt(nrm1 + eps) * gamma1)[None, :, None]
        return jnp.concatenate([n0, n1.reshape(n, 3 * C)], -1)
    edge_index = jnp.stack([src, dst])
    x = _layernorm(x + _L0_gnn_ref(x, edge_weight, src, dst), axis=-1)
    x = _layernorm(x + _L1_gnn_ref(x, edge_index, edge_attr_4, edge_attr_16, L1_gnn_W_up0, L1_gnn_W_up1, L1_gnn_M1, L1_gnn_M2, L1_gnn_M3, L1_gnn_M4, L1_gnn_W_lin0, L1_gnn_W_lin1, L1_gnn_Wsc0, L1_gnn_Wsc1, L1_gnn_Wc0, L1_gnn_Wc1, L1_gnn_WB0, L1_gnn_WB1, L1_gnn_gamma0, L1_gnn_beta0, L1_gnn_gamma1), axis=-1)
    return x

_drawn_inputs = setup_inputs


def setup_inputs(seed=0):
    import zlib

    import numpy as np

    out = dict(_drawn_inputs(seed))
    spreads = {'L1_gnn_gamma0': (1.0, 0.2), 'L1_gnn_beta0': (0.0, 0.1), 'L1_gnn_gamma1': (1.0, 0.2)}
    factors = {}
    for name, (base, spread) in spreads.items():
        noise = np.random.default_rng([zlib.crc32(name.encode()), seed]).standard_normal(out[name].shape)
        drawn = base * np.exp(spread * noise) if base else spread * noise
        out[name] = jnp.asarray(drawn.astype(out[name].dtype))
    for name, factor in factors.items():
        out[name] = (out[name] * factor).astype(out[name].dtype)
    return out
```

```python
from contextlib import ExitStack

import numpy as np

import concourse.bass as bass
import concourse.mybir as mybir

f32 = mybir.dt.float32
i32 = mybir.dt.int32
ALU = mybir.AluOpType
ACT = mybir.ActivationFunctionType

P = 128
D = 256
C = 64
TILES = 4
CHUNK = P * TILES
PAIR = 2 * P
REC = 4
STEPS = 512
OUT = D
EPS = 1e-5
SKIP = 1 << 20
TWO_PI = 2 * np.pi
TWO_PI_HI = 6.28125
TWO_PI_LO = TWO_PI - TWO_PI_HI
ROUND = 1.5 * 2.0 ** 23
BELOW_PI = 3.1415925
ABOVE_ALL = 4.0

K_IDENT, K_DUP, K_LOW, K_HIGH, K_ONES, K_TRI, K_EYE2, K_PLANES = 0, 128, 256, 384, 512, 640, 768, 832
K_ROW127 = K_PLANES + 2 * D
K_ROW = K_ROW127 + P
K_DOWN = K_ROW + 2
K_ALL = K_DOWN + STEPS + 1


class Named:
    pass


def tensors(nc, ctx, shapes):
    n_chunks, n_pairs = shapes["chunks"], shapes["pairs"]

    def sb(name, shape, dt=f32):
        return ctx.enter_context(nc.sbuf_tensor(name, shape, dt))

    t = Named()
    t.chunks, t.pairs, t.nodes = n_chunks, n_pairs, shapes["nodes"]
    t.const = sb("const", [P, K_ALL])
    t.matT = sb("matT", [P, 2, D])
    t.mix = sb("mix", [P, 2, D])
    t.mixT = sb("mixT", [P, 2, D])
    t.rstd1 = sb("rstd1", [P, n_chunks * TILES])
    t.gram = sb("gram", [P, 1 + 2 * P])
    t.edge_sums = sb("edge_sums", [1, 3 * C])
    t.scale = sb("scale", [P, D])
    t.shift = sb("shift", [P, D])
    t.shift_c = sb("shift_c", [P, D])
    t.fold = sb("fold", [P, 2, D])
    t.eps = sb("eps", [P, 1])
    t.hidden = sb("hidden", [P, n_pairs, P])
    t.bd = sb("bd", [P, 8, P])
    t.m1 = sb("m1", [32, P])
    t.m23 = sb("m23", [P, 2, P])
    t.m4 = sb("m4", [P, D])
    t.wstk = sb("wstk", [P, 2, C])
    t.wc = sb("wc", [P, 9])
    t.gb = sb("gb", [P, 3, C])
    t.edge_idx = sb("edge_idx", [P, 3, 2 * n_pairs], i32)
    t.edge_sh = sb("edge_sh", [P, 2 * n_pairs, 4])
    t.dstf = sb("dstf", [P, 2 * n_pairs])
    t.last = sb("last", [P, 2 * n_pairs])
    t.put = sb("put", [P, 2 * n_pairs], i32)
    return t


def prepare(nc, d, t):
    n_pairs = t.pairs
    COLS = 2 * n_pairs
    with ExitStack() as ctx:
        def sb(name, shape, dt=f32):
            return ctx.enter_context(nc.sbuf_tensor(name, shape, dt))

        def ps(name, shape):
            return ctx.enter_context(nc.psum_tensor(name, shape, f32))

        def sem(name):
            return ctx.enter_context(nc.semaphore(name))

        steps = sb("steps", [P, 3, COLS], i32)
        fij = sb("fij", [P, 2, COLS])
        inr = sb("inr", [P, 2, COLS])
        turns = sb("turns", [P, COLS])
        ang = sb("ang", [P, COLS])
        mag = sb("mag", [P, COLS])
        trig = sb("trig", [P, 2, COLS])
        act_m = sb("act_m", [P, COLS])
        zeros = sb("zeros", [P, COLS])
        run = sb("run", [P, COLS])
        pos_f = sb("pos_f", [P, COLS])
        pos = sb("pos", [P, COLS], i32)
        cnt_f = sb("cnt_f", [P, 1])
        n_sets = sb("n_sets", [P, 1], i32)
        rec = sb("rec", [P, COLS, REC])
        dummy = sb("unused_recs", [P, COLS, REC])
        half_pi = sb("half_pi", [P, 1])
        base = ps("base", [P, 512])
        rbf = sb("rbf", [32, 4, P])
        hid1 = sb("hid1", [P, 2, P])
        hid2 = sb("hid2", [P, 2, P])
        net = [ps(f"net{i}", [P, 512]) for i in range(3)]

        s_const = sem("s_const")
        s_steps = sem("s_steps")
        s_weights = sem("s_weights")
        s_prep = sem("s_prep")
        s_trig = sem("s_trig")
        s_half = sem("s_half")
        s_base = sem("s_base")
        s_recs = sem("s_recs")
        s_fill = sem("s_fill")
        s_dummy = sem("s_dummy")
        s_put = sem("s_put")
        s_at = sem("s_at")
        at = sb("at", [P, 4], i32)
        moved = sb("moved", [P, 4, REC])
        s_rbf = [sem(f"s_rbf{i}") for i in range(4)]
        s_net = [sem(f"s_net{i}") for i in range(3)]
        s_silu = [sem(f"s_silu{i}") for i in range(3)]
        s_edge = sem("s_edge")
        s_m4 = sem("s_m4")

        with nc.Block() as block:
            @block.sync
            def _(sp):
                sp.dma_start(steps[:, :, :], d.steps).then_inc(s_steps, 16)
                sp.dma_start(t.const[:, :], d.const).then_inc(s_const, 16)
                sp.dma_start(t.m1[:, :], d.m1).then_inc(s_weights, 16)
                sp.dma_start(t.m23[:, :, :], d.m23).then_inc(s_weights, 16)
                for p in range(4):
                    sp.dma_start(rbf[:, p, :], d.rbf[p]).then_inc(s_rbf[p], 16)
                sp.dma_start(t.bd[:, :, :], d.bd).then_inc(s_edge, 16)
                sp.dma_start(t.m4[:, :], d.m4).then_inc(s_edge, 16)
                sp.dma_start(t.wstk[:, :, :], d.wstk).then_inc(s_edge, 16)
                sp.dma_start(t.wc[:, :], d.wc).then_inc(s_edge, 16)
                sp.dma_start(t.gb[:, :, :], d.gb.partition_broadcast(P)).then_inc(s_edge, 16)
                sp.dma_start(t.edge_idx[:, :, :], d.edge_idx).then_inc(s_edge, 16)
                sp.dma_start(t.edge_sh[:, :, :], d.edge_sh).then_inc(s_edge, 16)

                def load_rbf(p, u, rnd):
                    sp.wait_ge(s_net[0], p - 3)
                    sp.dma_start(rbf[:, u, :], d.rbf[p]).then_inc(s_rbf[u], 16)

                with sp.Fori(1, n_pairs // 4) as it:
                    for u in range(4):
                        load_rbf(it * 4 + u, u, it)
                for p in range(n_pairs // 4 * 4, n_pairs):
                    load_rbf(p, p % 4, p // 4)

            @block.tensor
            def _(pe):
                pe.wait_ge(s_weights, 32)

                def layers(p, u, rnd, warm):
                    pe.wait_ge(s_rbf[u], rnd * 16 + 16)
                    if warm:
                        pe.wait_ge(s_silu[0], p)
                    nc.tensor.matmul(net[0][:, 0:P], t.m1[:, :], rbf[:, u, :], start=True, stop=True)\
                        .then_inc(s_net[0], 1)
                    pe.wait_ge(s_silu[0], p + 1)
                    if warm:
                        pe.wait_ge(s_silu[1], p)
                    nc.tensor.matmul(net[1][:, 0:P], t.m23[:, 0, :], hid1[:, u % 2, :], start=True, stop=True)\
                        .then_inc(s_net[1], 1)
                    pe.wait_ge(s_silu[1], p + 1)
                    if warm:
                        pe.wait_ge(s_silu[2], p)
                    nc.tensor.matmul(net[2][:, 0:P], t.m23[:, 1, :], hid2[:, u % 2, :], start=True, stop=True)\
                        .then_inc(s_net[2], 1)

                pe.wait_ge(s_const, 16)
                pe.wait_ge(s_prep, 1)
                nc.tensor.matmul(base[:, 0:1], t.const[:, K_TRI:K_TRI + P], run[:, COLS - 1:COLS],
                                 start=True, stop=True)
                nc.tensor.matmul(base[:, 1:2], t.const[:, K_ONES:K_ONES + P], run[:, COLS - 1:COLS],
                                 start=True, stop=True).then_inc(s_base, 1)
                for p in range(4):
                    layers(p, p, 0, p > 0)
                with pe.Fori(1, n_pairs // 4) as it:
                    for u in range(4):
                        layers(it * 4 + u, u, it, True)
                for p in range(n_pairs // 4 * 4, n_pairs):
                    layers(p, p % 4, p // 4, True)

            @block.scalar
            def _(act):
                act.wait_ge(s_half, 1)
                act.wait_ge(s_trig, 1)
                nc.scalar.activation(trig[:, 1, :], ang[:, :], ACT.Sin).then_inc(s_trig, 1)
                nc.scalar.activation(trig[:, 0, :], mag[:, :], ACT.Sin, scale=-1.0, bias=half_pi[:, 0:1])\
                    .then_inc(s_trig, 1)

                def silus(p, u):
                    for n, out in enumerate((hid1[:, u % 2, :], hid2[:, u % 2, :], t.hidden[:, p, :])):
                        act.wait_ge(s_net[n], p + 1)
                        nc.scalar.activation(out, net[n][:, 0:P], ACT.Silu).then_inc(s_silu[n], 1)

                for p in range(4):
                    silus(p, p)
                with act.Fori(1, n_pairs // 4) as it:
                    for u in range(4):
                        silus(it * 4 + u, u)
                for p in range(n_pairs // 4 * 4, n_pairs):
                    silus(p, p % 4)

            @block.vector
            def _(v):
                v.memset(half_pi[:, :], np.pi / 2).then_inc(s_half, 1)
                v.memset(t.eps[:, :], EPS)
                v.memset(zeros[:, :], 0.0)
                v.memset(dummy[:, :, :], float(OUT)).then_inc(s_dummy, 1)
                v.wait_ge(s_steps, 16)
                v.tensor_copy(fij[:, :, :], steps[:, 0:2, :])
                v.tensor_scalar(turns[:, :], steps[:, 2, :].bitcast(f32), 1 / TWO_PI, ROUND, ALU.mult, ALU.add)
                v.drain()
                v.tensor_scalar(inr[:, :, :], fij[:, :, :], float(D), None, ALU.is_lt)
                v.tensor_scalar(turns[:, :], turns[:, :], ROUND, None, ALU.subtract)
                v.drain()
                v.tensor_tensor(act_m[:, :], inr[:, 0, :], inr[:, 1, :], ALU.max)
                v.scalar_tensor_tensor(ang[:, :], turns[:, :], -TWO_PI_HI, steps[:, 2, :].bitcast(f32),
                                       ALU.mult, ALU.add)
                v.drain()
                v.tensor_tensor_scan(run[:, :], act_m[:, :], zeros[:, :], 0.0, ALU.add, ALU.add).then_inc(s_prep, 1)
                v.scalar_tensor_tensor(ang[:, :], turns[:, :], -TWO_PI_LO, ang[:, :], ALU.mult, ALU.add)
                v.tensor_scalar(rec[:, :, 0:2].rearrange("p c w -> p w c"), fij[:, :, :], float(OUT), None, ALU.min)
                v.drain()
                v.tensor_scalar(ang[:, :], ang[:, :], BELOW_PI, -BELOW_PI, ALU.min, ALU.max)
                v.drain()
                v.scalar_tensor_tensor(mag[:, :], ang[:, :], -1.0, ang[:, :], ALU.mult, ALU.max).then_inc(s_trig, 1)
                v.wait_ge(s_trig, 3)
                v.tensor_copy(rec[:, :, 2:4].rearrange("p c w -> p w c"), trig[:, :, :])
                v.wait_ge(s_base, 1)
                v.tensor_scalar(pos_f[:, :], run[:, :], base[:, 0:1], float(SKIP - 1), ALU.add, ALU.add)
                v.tensor_scalar(cnt_f[:, :], base[:, 1:2], 1 / STEPS, 0.5 - 1 / (4 * STEPS), ALU.mult, ALU.add)
                v.drain()
                v.scalar_tensor_tensor(pos[:, :], act_m[:, :], -float(SKIP), pos_f[:, :], ALU.mult, ALU.add)
                v.tensor_scalar(cnt_f[:, :], cnt_f[:, :], ROUND, None, ALU.add)
                v.drain()
                v.tensor_scalar(n_sets[:, :], cnt_f[:, :], ROUND, 1.0, ALU.subtract, ALU.max)
                v.drain().then_inc(s_recs, 1)
                v.wait_ge(s_edge, 112)
                v.tensor_copy(t.dstf[:, :], t.edge_idx[:, 1, :])
                v.tensor_tensor(t.last[:, :], t.edge_idx[:, 1, :], t.edge_idx[:, 2, :], ALU.not_equal)
                v.tensor_scalar(t.m4[:, 3 * C:4 * C], t.m4[:, 3 * C:4 * C], float(1 / np.sqrt(3.0)), None, ALU.mult)
                v.drain()
                v.tensor_scalar(pos_f[:, :], t.last[:, :], -float(SKIP), float(SKIP), ALU.mult, ALU.add)
                v.drain()
                v.tensor_tensor(t.put[:, :], pos_f[:, :], t.dstf[:, :], ALU.add)
                v.drain()

            @block.gpsimd
            def _(pool):
                bound = pool.to_reg(P * COLS - 1)
                pool.wait_ge(s_dummy, 1)
                pool.dma_start(d.recs.rearrange("(p c) w -> p c w", p=P), dummy[:, :, :]).then_inc(s_put, 16)
                pool.wait_ge(s_recs, 1)
                pool.dma_start(d.n_sets, n_sets[0:1, :]).then_inc(s_fill, 16)
                with pool.Fori(0, COLS // 4) as it:
                    pool.wait_ge(s_put, it * 64 + 16)
                    pool.tensor_copy(at[:, :], pos[:, bass.ds(it * 4, 4)]).then_inc(s_at, 1)
                    pool.tensor_copy(moved[:, :, :], rec[:, bass.ds(it * 4, 4), :]).then_inc(s_at, 1)
                    pool.wait_ge(s_at, it * 2 + 2)
                    pool.sem_inc(s_prep, 1)
                    for c in range(4):
                        pool.indirect_dma_start(d.recs, bass.IndirectOffsetOnAxis(ap=at[:, c:c + 1], axis=0),
                                                moved[:, c, :], None, bounds_check=bound,
                                                oob_is_err=False).then_inc(s_put, 16)
                pool.wait_ge(s_put, 16 * COLS + 16)
                pool.wait_ge(s_fill, 16)


def rotate(nc, d, t):
    with ExitStack() as ctx:
        def sb(name, shape, dt=f32):
            return ctx.enter_context(nc.sbuf_tensor(name, shape, dt))

        def sem(name):
            return ctx.enter_context(nc.semaphore(name))

        recs = sb("recs_sb", [P, STEPS + 1, REC])
        count = sb("count", [1, 1], i32)
        wide = sb("wide", [P, 3, STEPS + 1])
        plain = sb("plain", [P, STEPS])
        trig = sb("plain_trig", [P, 2, STEPS])
        hit = sb("hit", [P, 2, STEPS])
        signed = sb("signed", [P, 2, STEPS])
        coef = sb("coef", [P, 2, STEPS])
        kept = sb("kept", [P, 2, STEPS])
        add = sb("add", [P, 2, STEPS])
        pmap = sb("pmap", [P, 2, STEPS + 1])
        qmap = sb("qmap", [P, 2, STEPS + 1])
        left = sb("left", [P, STEPS + 1])
        first = sb("first", [P, 1])
        at = sb("at_end", [P, 1], i32)
        ends = sb("ends", [P, 2])
        ends_i = sb("ends_i", [P, 2], i32)
        is_ij = sb("is_ij", [P, 2, 2])
        pick = sb("pick", [P, 2, 2, P])
        abc = sb("abc", [P, 3, 2])
        part = sb("part", [P, 2, 2])
        clamped = sb("clamped_at", [P, 2])
        read = sb("read", [P, 2, 2])
        only_i = sb("only_i", [P, 2])
        rest = sb("rest", [P, 2, D])
        mat = sb("mat", [P, 2, D])
        row255 = ctx.enter_context(nc.psum_tensor("row255", [P, 512], f32))
        rows_ij = ctx.enter_context(nc.psum_tensor("rows_ij", [P, 2, D], f32))
        tp = ctx.enter_context(nc.psum_tensor("tp_mat", [P, 2, D], f32))
        s_loaded = sem("s_loaded")
        s_count, s_used, s_ends, s_mat, s_255, s_mapped, s_ij, s_done, s_tp, s_go = map(
            sem, ("s_count", "s_used", "s_ends", "s_mat", "s_255", "s_mapped", "s_ij", "s_mat_done", "s_tp_mat",
                  "s_go_set"))
        sets = d.recs[0:t.pairs * PAIR, :].rearrange("(s k) w -> s (k w)", k=STEPS)
        max_sets = t.pairs * PAIR // STEPS

        with nc.Block() as block:
            @block.sync
            def _(sp):
                sp.dma_start(count[:, :], d.n_sets).then_inc(s_count, 16)
                sp.wait_ge(s_count, 16)
                n = sp.value_load(count[0:1, 0:1], min_val=1, max_val=max_sets)
                with sp.Fori(0, n) as s:
                    sp.wait_ge(s_used, s + 1)
                    sp.dma_start(recs[:, 0:STEPS, :].rearrange("p k w -> p (k w)"),
                                 sets[s].partition_broadcast(P)).then_inc(s_loaded, 16)

            @block.tensor
            def _(pe):
                pe.wait_ge(s_count, 16)
                n = pe.value_load(count[0:1, 0:1], min_val=1, max_val=max_sets)
                with pe.Fori(0, n) as s:
                    pe.wait_ge(s_ends, s + 1)
                    pe.sem_inc(s_go, 1)
                    g0 = pe.value_load(ends_i[0:1, 0:1], min_val=0, max_val=t.pairs * PAIR + max_sets)
                    g1 = pe.value_load(ends_i[0:1, 1:2], min_val=0, max_val=t.pairs * PAIR + max_sets)
                    with pe.Fori(g0, g1) as g:
                        pe.wait_ge(s_mat, g + 1)
                        nc.tensor.matmul(row255[:, 0:D], t.const[:, K_ROW127:K_ROW127 + P], mat[:, 1, :],
                                         start=True, stop=True).then_inc(s_255, 1)
                        pe.wait_ge(s_mapped, g + 1)
                        for ij in range(2):
                            for b in range(2):
                                last = nc.tensor.matmul(rows_ij[:, ij, :], pick[:, ij, b, :], mat[:, b, :],
                                                        start=b == 0, stop=b == 1)
                        last.then_inc(s_ij, 1)
                pe.wait_ge(s_done, 1)
                for lb in range(2):
                    for kb in range(2):
                        last = nc.tensor.transpose(tp[:, lb, kb * P:(kb + 1) * P], mat[:, kb, lb * P:(lb + 1) * P],
                                                   t.const[:, K_IDENT:K_IDENT + P])
                last.then_inc(s_tp, 1)

            @block.vector
            def _(v):
                v.memset(ends[:, :], 0.0).then_inc(s_used, 1)
                v.memset(mat[:, :, :], 0.0)
                v.memset(pmap[:, :, 0:1], 1.0)
                v.memset(qmap[:, :, 0:1], 0.0)
                v.memset(wide[:, 0, STEPS:STEPS + 1], 1.0)
                v.memset(recs[:, STEPS, :], float(OUT))
                v.drain()
                for b in range(2):
                    last = v.tensor_copy(mat[:, b, b * P:(b + 1) * P], t.const[:, K_IDENT:K_IDENT + P])
                last.then_inc(s_mat, 1)
                v.wait_ge(s_count, 16)
                n = v.value_load(count[0:1, 0:1], min_val=1, max_val=max_sets)
                ri, rj, rcos, rsin = (recs[:, 0:STEPS, k] for k in range(4))
                kid = [t.const[:, K_ROW + b:K_ROW + b + 1] for b in range(2)]
                with v.Fori(0, n) as s:
                    v.wait_ge(s_loaded, s * 16 + 16)
                    v.tensor_tensor(wide[:, 1, 0:STEPS], ri, rj, ALU.max)
                    v.tensor_scalar(wide[:, 2, 0:STEPS], ri, float(D - 1), None, ALU.is_equal)
                    v.drain()
                    v.tensor_scalar(wide[:, 1, 0:STEPS], wide[:, 1, 0:STEPS], float(D), None, ALU.is_lt)
                    v.scalar_tensor_tensor(wide[:, 2, 0:STEPS], rj, float(D - 1), wide[:, 2, 0:STEPS],
                                           ALU.is_equal, ALU.max)
                    for b in range(2):
                        v.tensor_scalar(hit[:, b, :], ri, kid[b], None, ALU.is_equal)
                    v.drain()
                    v.tensor_tensor(wide[:, 0, 0:STEPS], wide[:, 1, 0:STEPS], wide[:, 2, 0:STEPS], ALU.max)
                    for b in range(2):
                        v.scalar_tensor_tensor(signed[:, b, :], rj, kid[b], hit[:, b, :], ALU.is_equal, ALU.subtract)
                    v.drain()
                    v.tensor_scalar(plain[:, :], wide[:, 0, 0:STEPS], -1.0, 1.0, ALU.mult, ALU.add)
                    for b in range(2):
                        v.scalar_tensor_tensor(hit[:, b, :], rj, kid[b], hit[:, b, :], ALU.is_equal, ALU.add)
                    v.tensor_tensor(left[:, :], wide[:, 0, :], t.const[:, K_DOWN:K_DOWN + STEPS + 1], ALU.mult)
                    v.reduce_sum(ends[:, 1:2], wide[:, 0, :], axis=mybir.AxisListType.X)
                    v.drain()
                    v.tensor_tensor(trig[:, 0, :], rcos, plain[:, :], ALU.mult)
                    v.tensor_tensor(trig[:, 1, :], rsin, plain[:, :], ALU.mult)
                    v.tensor_tensor(ends[:, 1:2], ends[:, 1:2], ends[:, 0:1], ALU.add)
                    v.drain()
                    v.tensor_copy(ends_i[:, :], ends[:, :])
                    for b in range(2):
                        v.tensor_tensor(add[:, b, :], signed[:, b, :], trig[:, 1, :], ALU.mult)
                    for b in range(2):
                        v.scalar_tensor_tensor(coef[:, b, :], hit[:, b, :], 0.0, plain[:, :], ALU.is_equal, ALU.mult)
                        v.tensor_tensor(kept[:, b, :], hit[:, b, :], trig[:, 0, :], ALU.mult)
                    v.drain().then_inc(s_ends, 1)
                    for b in range(2):
                        v.tensor_tensor(coef[:, b, :], coef[:, b, :], kept[:, b, :], ALU.add)
                    v.tensor_copy(ends[:, 0:1], ends[:, 1:2])
                    v.drain()
                    for b in range(2):
                        v.tensor_tensor_scan(pmap[:, b, 1:STEPS + 1], coef[:, b, :], wide[:, 0, 0:STEPS], 1.0,
                                             ALU.mult, ALU.add)
                        v.tensor_tensor_scan(qmap[:, b, 1:STEPS + 1], coef[:, b, :], add[:, b, :], 0.0,
                                             ALU.mult, ALU.add)
                    g0 = v.value_load(ends_i[0:1, 0:1], min_val=0, max_val=t.pairs * PAIR + max_sets)
                    g1 = v.value_load(ends_i[0:1, 1:2], min_val=0, max_val=t.pairs * PAIR + max_sets)
                    with v.Fori(g0, g1) as g:
                        v.reduce_max(first[:, :], left[:, :], axis=mybir.AxisListType.X)
                        v.drain()
                        v.tensor_scalar(at[:, :], first[:, :], -1.0, float(STEPS + 1), ALU.mult, ALU.add)
                        v.scalar_tensor_tensor(left[:, :], left[:, :], first[:, 0:1], left[:, :], ALU.is_lt, ALU.mult)
                        v.drain()
                        k = v.value_load(at[0:1, 0:1], min_val=0, max_val=STEPS)
                        i_at, j_at, cos_at, sin_at = (recs[:, bass.ds(k, 1), w] for w in range(4))
                        rows = t.const[:, K_ROW:K_ROW + 2]
                        for ij in range(2):
                            v.tensor_scalar(is_ij[:, ij, :], rows, (i_at, j_at)[ij], None, ALU.is_equal)
                        v.tensor_scalar(clamped[:, :].unsqueeze(1), recs[:, bass.ds(k, 1), 0:2], float(D - 1), None,
                                        ALU.min)
                        v.drain()
                        for ij in range(2):
                            v.tensor_scalar(read[:, ij, :], rows, clamped[:, ij:ij + 1], None, ALU.is_equal)
                        v.scalar_tensor_tensor(only_i[:, :], is_ij[:, 1, :], 0.0, is_ij[:, 0, :],
                                               ALU.is_equal, ALU.mult)
                        v.tensor_scalar(part[:, 0, :], is_ij[:, 1, :], sin_at, None, ALU.mult)
                        v.drain()
                        for ij in range(2):
                            for b in range(2):
                                v.tensor_scalar(pick[:, ij, b, :], t.const[:, K_ONES:K_ONES + P],
                                                read[:, ij, b:b + 1], None, ALU.mult)
                        v.tensor_scalar(part[:, 1, :], only_i[:, :], sin_at, None, ALU.mult)
                        v.tensor_tensor(abc[:, 2, :], only_i[:, :], is_ij[:, 1, :], ALU.add)
                        v.drain()
                        v.scalar_tensor_tensor(abc[:, 0, :], only_i[:, :], cos_at, part[:, 0, :], ALU.mult, ALU.add)
                        v.scalar_tensor_tensor(abc[:, 1, :], is_ij[:, 1, :], cos_at, part[:, 1, :], ALU.mult,
                                               ALU.subtract)
                        v.tensor_scalar(abc[:, 2, :], abc[:, 2, :], -1.0, 1.0, ALU.mult, ALU.add)
                        for b in range(2):
                            v.tensor_scalar(rest[:, b, :], mat[:, b, :], pmap[:, b, bass.ds(k, 1)], None, ALU.mult)
                        v.drain()
                        v.wait_ge(s_255, g + 1)
                        for b in range(2):
                            v.scalar_tensor_tensor(mat[:, b, :], row255[:, 0:D], qmap[:, b, bass.ds(k, 1)],
                                                   rest[:, b, :], ALU.mult, ALU.add)
                        v.drain().then_inc(s_mapped, 1)
                        for b in range(2):
                            v.tensor_scalar(rest[:, b, :], mat[:, b, :], abc[:, 2, b:b + 1], None, ALU.mult)
                        v.drain()
                        v.wait_ge(s_ij, g + 1)
                        for ij in range(2):
                            for b in range(2):
                                v.scalar_tensor_tensor((rest, mat)[ij][:, b, :], rows_ij[:, ij, :],
                                                       abc[:, ij, b:b + 1], rest[:, b, :], ALU.mult, ALU.add)
                            v.drain()
                        v.sem_inc(s_mat, 1)
                    v.drain().then_inc(s_used, 1)
                v.sem_inc(s_done, 1)
                v.wait_ge(s_tp, 1)
                v.tensor_copy(t.matT[:, :, :], tp[:, :, :])
                v.drain()


def mix_matrix(nc, t):
    with ExitStack() as ctx:
        mean = ctx.enter_context(nc.sbuf_tensor("mean", [P, 2], f32))
        tp = ctx.enter_context(nc.psum_tensor("tp", [P, 2, D], f32))
        s_mix = ctx.enter_context(nc.semaphore("s_mix"))
        s_tp = ctx.enter_context(nc.semaphore("s_tp"))
        with nc.Block() as block:
            @block.vector
            def _(v):
                for lb in range(2):
                    eye = t.const[:, K_PLANES + lb * D:K_PLANES + (lb + 1) * D]
                    v.tensor_tensor(t.mix[:, lb, 0:C], t.matT[:, lb, 0:C], eye[:, 0:C], ALU.add)
                    for x in range(3):
                        plane = slice(C * (1 + x), C * (2 + x))
                        v.tensor_tensor(t.mix[:, lb, plane], t.matT[:, lb, C + x:D:3], eye[:, plane], ALU.add)
                v.drain()
                v.reduce_sum(mean[:, :], t.mix[:, :, :], axis=mybir.AxisListType.X)
                v.drain()
                v.tensor_scalar(mean[:, :], mean[:, :], 1 / D, None, ALU.mult)
                v.drain()
                for lb in range(2):
                    v.tensor_scalar(t.mix[:, lb, :], t.mix[:, lb, :], mean[:, lb:lb + 1], None, ALU.subtract)\
                        .then_inc(s_mix, 1)
                v.wait_ge(s_tp, 1)
                v.tensor_copy(t.mixT[:, :, :], tp[:, :, :])
                v.drain()

            @block.tensor
            def _(pe):
                pe.wait_ge(s_mix, 2)
                for cb in range(2):
                    for lb in range(2):
                        last = nc.tensor.transpose(tp[:, cb, lb * P:(lb + 1) * P],
                                                   t.mix[:, lb, cb * P:(cb + 1) * P],
                                                   t.const[:, K_IDENT:K_IDENT + P])
                last.then_inc(s_tp, 1)


def node_stats(nc, d, t):
    n = t.chunks
    SLOTS = 4
    rows = d.h.rearrange("(c i p) f -> c p i f", i=TILES, p=P)
    with ExitStack() as ctx:
        def sb(name, shape, dt=f32):
            return ctx.enter_context(nc.sbuf_tensor(name, shape, dt))

        def ps(name, shape):
            return ctx.enter_context(nc.psum_tensor(name, shape, f32))

        def sem(name):
            return ctx.enter_context(nc.semaphore(name))

        xT = sb("xT", [P, SLOTS, 2, CHUNK])
        h = sb("h_sb", [P, SLOTS, TILES, 1 + D])
        squares = sb("squares", [P, TILES, D])
        ss = sb("ss", [P, SLOTS, TILES])
        std = sb("std", [P, SLOTS, TILES])
        var = sb("var", [P, SLOTS, TILES])
        inv = sb("inv", [P, SLOTS, TILES])
        near = sb("near", [P, SLOTS, TILES])
        corr = sb("corr", [P, SLOTS, TILES])
        y = ps("y", [P, 2, TILES, D])
        gram_a = ps("gram_a", [P, 512])
        gram_b = ps("gram_b", [P, 512])
        s_x = [sem(f"s_x{i}") for i in range(SLOTS)]
        s_hout = [sem(f"s_hout{i}") for i in range(SLOTS)]
        s_y, s_ss, s_std, s_r, s_h, s_gram, s_ones = map(
            sem, ("s_y", "s_ss", "s_std", "s_r", "s_h", "s_gram", "s_ones"))

        with nc.Block() as block:
            @block.sync
            def _(sp):
                for c in range(SLOTS):
                    sp.dma_start(xT[:, c], d.xT[c]).then_inc(s_x[c], 16)

                def turn(c, u, load=True):
                    if load:
                        sp.wait_ge(s_y, (c + 1) * TILES)
                        sp.dma_start(xT[:, u], d.xT[c + SLOTS]).then_inc(s_x[u], 16)
                    sp.wait_ge(s_h, c + 1)
                    sp.dma_start(rows[c], h[:, u, :, 1:1 + D]).then_inc(s_hout[u], 16)

                with sp.Fori(0, n // SLOTS - 1) as it:
                    for u in range(SLOTS):
                        turn(it * SLOTS + u, u)
                for c in range(n - SLOTS, n):
                    turn(c, c % SLOTS, load=False)
                for u in range(SLOTS):
                    sp.wait_ge(s_hout[u], n // SLOTS * 16)

            @block.tensor
            def _(pe):
                def products(c, u, rnd, warm=True):
                    pe.wait_ge(s_x[u], rnd * 16 + 16)
                    if warm:
                        pe.wait_ge(s_h, c - 1)
                    for i in range(TILES):
                        for lb in range(2):
                            last = nc.tensor.matmul(y[:, u % 2, i, :], xT[:, u, lb, i * P:(i + 1) * P],
                                                    t.mix[:, lb, :], start=lb == 0, stop=lb == 1)
                        last.then_inc(s_y, 1)

                def gram(c, u, start=False, stop=False):
                    pe.wait_ge(s_h, c + 1)
                    for i in range(TILES):
                        nc.tensor.matmul(gram_a[:, 0:1 + P], h[:, u, i, 1:1 + P], h[:, u, i, 0:1 + P],
                                         start=start and i == 0, stop=stop and i == TILES - 1)
                        last = nc.tensor.matmul(gram_b[:, 0:P], h[:, u, i, 1 + P:1 + D], h[:, u, i, 1 + P:1 + D],
                                                start=start and i == 0, stop=stop and i == TILES - 1)
                    last.then_inc(s_gram, 1)

                pe.wait_ge(s_ones, 1)
                for c in range(SLOTS):
                    products(c, c, 0, c >= 2)
                    if c >= 2:
                        gram(c - 2, c - 2, start=c == 2)
                with pe.Fori(1, n // SLOTS) as it:
                    for u in range(SLOTS):
                        products(it * SLOTS + u, u, it)
                        gram(it * SLOTS + u - 2, (u - 2) % SLOTS)
                gram(n - 2, (n - 2) % SLOTS)
                gram(n - 1, (n - 1) % SLOTS, stop=True)

            @block.scalar
            def _(act):
                def turn(c, u):
                    for i in range(TILES):
                        act.wait_ge(s_y, c * TILES + i // 2 * 2 + 2)
                        nc.scalar.activation(squares[:, i, :], y[:, u % 2, i, :], ACT.Square,
                                             accum_out=ss[:, u, i:i + 1]).then_inc(s_ss, 1)
                    act.wait_ge(s_ss, c * TILES + TILES)
                    nc.scalar.activation(std[:, u, :], ss[:, u, :], ACT.Sqrt, scale=1 / D, bias=t.eps[:, 0:1])\
                        .then_inc(s_std, 1)

                with act.Fori(0, n // SLOTS) as it:
                    for u in range(SLOTS):
                        turn(it * SLOTS + u, u)

            @block.vector
            def _(v):
                v.memset(h[:, :, :, 0:1], 1.0).then_inc(s_ones, 1)

                def turn(c, u):
                    v.wait_ge(s_ss, c * TILES + TILES)
                    v.tensor_scalar(var[:, u, :], ss[:, u, :], 1 / D, EPS, ALU.mult, ALU.add).then_inc(s_r, 1)
                    v.wait_ge(s_std, c + 1)
                    v.reciprocal(inv[:, u, :], std[:, u, :]).then_inc(s_r, 1)
                    v.wait_ge(s_r, c * 5 + 2)
                    v.tensor_tensor(near[:, u, :], inv[:, u, :], var[:, u, :], ALU.mult).then_inc(s_r, 1)
                    v.wait_ge(s_r, c * 5 + 3)
                    v.scalar_tensor_tensor(corr[:, u, :], near[:, u, :], -0.5, inv[:, u, :], ALU.mult, ALU.mult)\
                        .then_inc(s_r, 1)
                    v.wait_ge(s_r, c * 5 + 4)
                    v.scalar_tensor_tensor(t.rstd1[:, bass.ds(c * TILES, TILES)], corr[:, u, :], 1.5, inv[:, u, :],
                                           ALU.add, ALU.mult).then_inc(s_r, 1)
                    v.wait_ge(s_r, c * 5 + 5)
                    for i in range(TILES):
                        last = v.tensor_scalar(h[:, u, i, 1:1 + D], y[:, u % 2, i, :],
                                               t.rstd1[:, bass.ds(c * TILES + i, 1)], None, ALU.mult)
                    last.then_inc(s_h, 1)

                for c in range(SLOTS):
                    turn(c, c)
                with v.Fori(1, n // SLOTS) as it:
                    for u in range(SLOTS):
                        v.wait_ge(s_hout[u], it * 16)
                        v.wait_ge(s_gram, it * SLOTS + (u - SLOTS + 1))
                        turn(it * SLOTS + u, u)
                v.wait_ge(s_gram, n)
                v.tensor_copy(t.gram[:, 0:1 + P], gram_a[:, 0:1 + P])
                v.tensor_copy(t.gram[:, 1 + P:1 + 2 * P], gram_b[:, 0:P])
                v.drain()


def staged(eng, n, unroll, stages):
    lags = [lag for lag, _ in stages]
    low, high = min(min(lags), 0), max(lags)

    first = -(-(high + unroll) // unroll) * unroll
    end = (n + low) // unroll * unroll

    def turn(p, u):
        for lag, stage in stages:
            if not isinstance(p, int) or 0 <= p - lag < n:
                stage(p - lag, (u - lag) % unroll)

    for p in range(low, min(first, end)):
        turn(p, p % unroll)
    if end > first:
        with eng.Fori(first // unroll, end // unroll) as it:
            for u in range(unroll):
                turn(it * unroll + u, u)
    for p in range(end, n + high):
        turn(p, p % unroll)


def before(p, k=1):
    return not isinstance(p, int) or p >= k


def of_slot(p, u, per=16, unroll=2):
    return (p // unroll + 1) * per if isinstance(p, int) else (p - u) * (per // unroll) + per


def edges(nc, d, t):
    n = t.pairs
    with ExitStack() as ctx:
        def sb(name, shape, dt=f32):
            return ctx.enter_context(nc.sbuf_tensor(name, shape, dt))

        def ps(name, shape):
            return ctx.enter_context(nc.psum_tensor(name, shape, f32))

        def sem(name):
            return ctx.enter_context(nc.semaphore(name))

        hs = sb("hs", [P, 2, 2, D])
        hd = sb("hd", [P, 2, 2, 1 + D])
        marked = sb("marked", [P, 2, 1 + D])
        rowd = sb("rowd", [P, 2, 1 + PAIR], i32)
        at_s = sb("at_s", [P, 2, 2], i32)
        at_d = sb("at_d", [P, 2, 2], i32)
        hsT = sb("hsT", [P, 2, 2, P])
        hdT = sb("hdT", [P, 2, 2, P])
        lhid = sb("lhid", [P, 2, P])
        tpw = sb("tpw", [P, 2, 4, C])
        xs0 = sb("xs0", [P, 2, C])
        dx = sb("dx", [P, 2, 3, C])
        dot = sb("dot", [P, 2, C])
        ma = sb("ma", [P, 2, C])
        mb = sb("mb", [P, 2, C])
        pp = sb("pp", [P, 2, C])
        qq = sb("qq", [P, 2, C])
        mp = sb("mp", [P, 2, 3, C])
        mq = sb("mq", [P, 2, 3, C])
        msg = sb("msg", [P, 2, 2, 4, C])
        eq0 = sb("eq0", [P, 2, PAIR])
        own = sb("own", [P, 2, 2])
        eq1 = sb("eq1", [P, 2, P])
        ind = sb("ind", [P, 2, P])
        sumT = sb("sumT", [P, 2, 4, P])
        linT = sb("linT", [P, 4, P])
        sq = sb("sq", [P, 3, P])
        aff = sb("aff", [P, 2, P])
        vv = sb("vv", [P, P])
        pb = sb("pb", [P, P])
        pg = sb("pg", [P, P])
        basT = sb("basT", [P, 2, 4, P])
        o_sb = sb("o_sb", [P, 2, 2, D])
        sqo = sb("sqo", [P, 2, D])
        p_t = ps("p_t", [P, 2, 2, P])
        p_tpw = ps("p_tpw", [P, 2, 4, C])
        p_up = ps("p_up", [P, 2, 4, C])
        p_sum = ps("p_sum", [P, 4, P])
        p_lin = ps("p_lin", [P, 4, P])
        p_o = ps("p_o", [P, 2, D])
        p_carry = ps("p_carry", [P, 512])
        p_stat = ps("p_stat", [P, 512])

        s_hs = [sem(f"s_hs{i}") for i in range(2)]
        s_hd = [sem(f"s_hd{i}") for i in range(2)]
        s_row = [sem(f"s_row{i}") for i in range(2)]
        s_oout = [sem(f"s_oout{i}") for i in range(2)]
        s_hdout = [sem(f"s_hdout{i}") for i in range(2)]
        q = Named()
        (q.ths, q.hsT, q.thd, q.hdT, q.lhid, q.ptpw, q.tpw, q.up, q.m, q.msg, q.gram, q.eq, q.own, q.ind, q.psum, q.carry, q.sum,
         q.plin, q.lin, q.bas, q.self, q.marked, q.o, q.osb, q.sq, q.stat, q.ats, q.atd, q.clear, q.go) = map(
            sem, ("s_ths", "s_hsT", "s_thd", "s_hdT", "s_lhid", "s_ptpw", "s_tpw", "s_up", "s_m", "s_msg",
                  "s_gram_recv", "s_eq", "s_own", "s_ind", "s_psum", "s_carry", "s_sum", "s_plin", "s_lin", "s_bas", "s_self", "s_marked", "s_o",
                  "s_osb", "s_sq", "s_stat", "s_ats", "s_atd", "s_clear", "s_go"))
        ident = t.const[:, K_IDENT:K_IDENT + P]
        UP, SELF, LIN, WB = 0, 2, 4, 6

        with nc.Block() as block:
            @block.sync
            def _(sp):
                def rows_in(p, u):
                    if before(p, 2):
                        sp.wait_ge(q.eq, p - 1)
                        sp.wait_ge(q.ind, p - 1)
                    sp.dma_start(rowd[:, u, :], d.dst_row[bass.ds(p * PAIR, 1 + PAIR)].partition_broadcast(P))\
                        .then_inc(s_row[u], 16)

                def hd_out(p, u):
                    sp.wait_ge(s_hd[u], of_slot(p, u, 32))
                    sp.dma_start(d.hd[p], hd[:, u, :, 1:1 + D]).then_inc(s_hdout[u], 16)

                def o_out(p, u):
                    sp.wait_ge(q.osb, p + 1)
                    sp.dma_start(d.o[p], o_sb[:, u]).then_inc(s_oout[u], 16)

                staged(sp, n, 2, [(0, rows_in), (3, hd_out), (5, o_out)])
                for u in range(2):
                    sp.wait_ge(s_oout[u], n // 2 * 16)
                    sp.wait_ge(s_hdout[u], n // 2 * 16)

            @block.gpsimd
            def _(pool):
                bound = pool.to_reg(t.chunks * CHUNK - 1)

                def senders(p, u):
                    if before(p, 2):
                        pool.wait_ge(q.ths, p - 1)
                    pool.tensor_copy(at_s[:, u, :], t.edge_idx[:, 0, bass.ds(p * 2, 2)]).then_inc(q.ats, 1)
                    pool.wait_ge(q.ats, p + 1)
                    pool.sem_inc(q.go, 1)
                    for j in range(2):
                        pool.indirect_dma_start(
                            hs[:, u, j, :], None, d.h, bass.IndirectOffsetOnAxis(ap=at_s[:, u, j:j + 1], axis=0),
                            bounds_check=bound, oob_is_err=False).then_inc(s_hs[u], 16)

                def receivers(p, u):
                    if before(p, 2):
                        pool.wait_ge(s_hdout[u], of_slot(p - 2, u))
                        pool.wait_ge(q.gram, p - 1)
                    pool.tensor_copy(at_d[:, u, :], t.edge_idx[:, 1, bass.ds(p * 2, 2)]).then_inc(q.atd, 1)
                    pool.wait_ge(q.atd, p + 1)
                    pool.sem_inc(q.go, 1)
                    for j in range(2):
                        pool.indirect_dma_start(
                            hd[:, u, j, 1:1 + D], None, d.h, bass.IndirectOffsetOnAxis(ap=at_d[:, u, j:j + 1], axis=0),
                            bounds_check=bound, oob_is_err=False).then_inc(s_hd[u], 16)

                def masks(p, u):
                    if before(p, 2):
                        pool.wait_ge(q.psum, p - 1)
                    pool.tensor_copy(own[:, u, :], t.dstf[:, bass.ds(p * 2, 2)]).then_inc(q.own, 1)
                    pool.wait_ge(q.own, p + 1)
                    pool.wait_ge(s_row[u], of_slot(p, u))
                    pool.sem_inc(q.go, 1)
                    pool.tensor_scalar(eq0[:, u, :], rowd[:, u, 1:1 + PAIR], own[:, u, 0:1], None, ALU.is_equal)
                    pool.tensor_scalar(eq1[:, u, :], rowd[:, u, 1 + P:1 + PAIR], own[:, u, 1:2], None, ALU.is_equal)\
                        .then_inc(q.eq, 1)

                staged(pool, n, 2, [(-1, senders), (1, masks), (2, receivers)])

            @block.tensor
            def _(pe):
                def senders_T(p, u):
                    pe.wait_ge(s_hs[u], of_slot(p, u, 32))
                    if before(p, 4):
                        pe.wait_ge(q.hdT, p - 3)
                    for j in range(2):
                        for b in range(2):
                            last = nc.tensor.transpose(p_t[:, j, b, :], hs[:, u, j, b * P:(b + 1) * P], ident)
                    last.then_inc(q.ths, 1)

                def sums(p, u):
                    pe.wait_ge(q.msg, p + 1)
                    pe.wait_ge(q.eq, p + 1)
                    if before(p):
                        pe.wait_ge(q.sum, p)
                    for j in range(2):
                        own = eq0[:, u, 0:P] if j == 0 else eq1[:, u, :]
                        for x in range(4):
                            last = nc.tensor.matmul(p_sum[j * C:(j + 1) * C, x, :], msg[:, u, j, x, :], own,
                                                    start=True, stop=j == 0)
                            if j == 1:
                                last = nc.tensor.matmul(p_sum[C:2 * C, x, :], msg[:, u, 0, x, :],
                                                        eq0[:, u, P:PAIR], start=False, stop=True)
                    last.then_inc(q.psum, 1)

                def receivers_T(p, u):
                    pe.wait_ge(s_hd[u], of_slot(p, u, 32))
                    pe.wait_ge(q.hsT, p + 4 if not isinstance(p, int) else min(p + 4, n))
                    for j in range(2):
                        for b in range(2):
                            last = nc.tensor.transpose(p_t[:, j, b, :], hd[:, u, j, 1 + b * P:1 + (b + 1) * P], ident)
                    last.then_inc(q.thd, 1)

                def up(p, u):
                    pe.wait_ge(q.hsT, p + 1)
                    if before(p):
                        pe.wait_ge(q.m, p)
                    for j in range(2):
                        for b in range(2):
                            last = nc.tensor.matmul(p_up[:, j, 2 * b:2 * b + 2, :], hsT[:, j, b, :],
                                                    t.bd[:, UP + b, :], start=True, stop=True)
                    last.then_inc(q.up, 1)

                def weights(p, u):
                    pe.wait_ge(q.lhid, p + 1)
                    if before(p):
                        pe.wait_ge(q.tpw, p)
                    for j in range(2):
                        last = nc.tensor.matmul(p_tpw[:, j, :, :], lhid[:, j, :],
                                                t.m4[:, :], start=True, stop=True)
                    last.then_inc(q.ptpw, 1)

                def lin(p, u):
                    pe.wait_ge(q.sum, p + 1)
                    if before(p):
                        pe.wait_ge(q.lin, p)
                    nc.tensor.matmul(p_lin[:, 0, :], t.bd[:, LIN, :], sumT[:, u, 0, :], start=True, stop=True)
                    nc.tensor.matmul(p_lin[:, 1:4, :], t.bd[:, LIN + 1, :], sumT[:, u, 1:4, :],
                                     start=True, stop=True).then_inc(q.plin, 1)
                    nc.tensor.matmul(p_carry[:, 0:4], t.const[:, K_DUP:K_DUP + P], sumT[:, u, :, P - 1],
                                     start=True, stop=True).then_inc(q.carry, 1)

                def self_part(p, u):
                    pe.wait_ge(q.hdT, p + 1)
                    if before(p):
                        pe.wait_ge(q.osb, p)
                    for j in range(2):
                        for b in range(2):
                            last = nc.tensor.matmul(p_o[:, j, b * P:(b + 1) * P], hdT[:, j, b, :],
                                                    t.bd[:, SELF + b, :], start=j == 0 and b == 0, stop=False,
                                                    skip_group_check=True)
                    last.then_inc(q.self, 1)

                def basis_part(p, u):
                    pe.wait_ge(q.bas, p + 1)
                    for x in range(4):
                        last = nc.tensor.matmul(p_o[:, :, x * C:(x + 1) * C], basT[:, u, x, :],
                                                t.bd[:, WB + min(x, 1), :], start=False, stop=x == 3,
                                                skip_group_check=True)
                    last.then_inc(q.o, 1)

                def gram(p, u):
                    pe.wait_ge(q.marked, p + 1)
                    for j in range(2):
                        first = isinstance(p, int) and p == 0 and j == 0
                        for b in range(2):
                            of = hd[:, u, j, 1 + b * P:1 + (b + 1) * P]
                            nc.tensor.matmul(p_stat[:, b * P:(b + 1) * P], of, marked[:, j, 1 + b * P:1 + (b + 1) * P],
                                             start=first and b == 0, stop=False, skip_group_check=True)
                        last = nc.tensor.matmul(p_stat[:, D:D + 1], hd[:, u, j, 1:1 + P], marked[:, j, 0:1],
                                                start=False, stop=False, skip_group_check=True)
                    last.then_inc(q.gram, 1)

                def stat(p, u):
                    pe.wait_ge(q.sq, p + 1)
                    for j in range(2):
                        for at, of in ((0, sqo[:, j, 0:C]), (1, sqo[:, j, C:2 * C]), (1, sqo[:, j, 2 * C:3 * C]),
                                       (1, sqo[:, j, 3 * C:D]), (2, o_sb[:, u, j, 0:C])):
                            last = nc.tensor.matmul(p_stat[0:1, D + 1 + at * C:D + 1 + (at + 1) * C],
                                                    marked[:, j, 0:1], of, start=False, stop=False,
                                                    skip_group_check=True)
                    last.then_inc(q.stat, 1)

                staged(pe, n, 2, [(1, up), (1, weights), (5, stat), (4, self_part), (0, senders_T), (2, sums), (3, lin),
                            (4, gram), (3, receivers_T), (4, basis_part)])

            @block.scalar
            def _(act):
                def hidden(p, u):
                    if before(p):
                        act.wait_ge(q.ptpw, p)
                    for j in range(2):
                        half = slice(j * C, (j + 1) * C)
                        last = nc.scalar.activation(lhid[half, j:j + 1, :], t.hidden[half, bass.ds(p, 1), :], ACT.Copy)
                    last.then_inc(q.lhid, 1)

                def senders_out(p, u):
                    act.wait_ge(q.ths, p + 1)
                    if before(p):
                        act.wait_ge(q.up, p)
                    nc.scalar.activation(hsT[:, :, :, :], p_t[:, :, :, :], ACT.Copy).then_inc(q.hsT, 1)

                def weights_out(p, u):
                    act.wait_ge(q.ptpw, p + 1)
                    if before(p):
                        act.wait_ge(q.m, p)
                    nc.scalar.activation(tpw[:, :, :, :], p_tpw[:, :, :, :], ACT.Copy).then_inc(q.tpw, 1)

                def receivers_out(p, u):
                    act.wait_ge(q.thd, p + 1)
                    if before(p):
                        act.wait_ge(q.self, p)
                    nc.scalar.activation(hdT[:, :, :, :], p_t[:, :, :, :], ACT.Copy).then_inc(q.hdT, 1)

                def lin_out(p, u):
                    act.wait_ge(q.plin, p + 1)
                    if before(p):
                        act.wait_ge(q.bas, p)
                    nc.scalar.activation(linT[:, :, :], p_lin[:, :, :], ACT.Copy)
                    nc.scalar.activation(sq[:, :, :], p_lin[:, 1:4, :], ACT.Square)
                    for k in range(2):
                        last = nc.scalar.activation(aff[:, k, :], p_lin[:, 0, :], ACT.Identity,
                                                    scale=t.wc[:, k:k + 1], bias=t.wc[:, 2 + k:3 + k])
                    last.then_inc(q.lin, 1)

                def mark(p, u):
                    act.wait_ge(s_hd[u], of_slot(p, u, 32))
                    if before(p):
                        act.wait_ge(q.stat, p)
                    for j in range(2):
                        last = nc.scalar.activation(marked[:, j, :], hd[:, u, j, :], ACT.Copy,
                                                    scale=t.last[:, bass.ds(p * 2 + j, 1)])
                    last.then_inc(q.marked, 1)

                def out_out(p, u):
                    act.wait_ge(q.o, p + 1)
                    if before(p, 2):
                        act.wait_ge(s_oout[u], of_slot(p - 2, u))
                    if before(p):
                        act.wait_ge(q.stat, p)
                    nc.scalar.activation(o_sb[:, u, :, :], p_o[:, :, :], ACT.Copy).then_inc(q.osb, 1)
                    act.wait_ge(q.osb, p + 1)
                    nc.scalar.activation(sqo[:, :, :], o_sb[:, u, :, :], ACT.Square).then_inc(q.sq, 1)

                act.wait_ge(q.clear, 1)
                staged(act, n, 2, [(1, weights_out), (0, hidden), (4, mark), (0, senders_out), (3, lin_out),
                             (3, receivers_out), (4, out_out)])

            @block.vector
            def _(v):
                def continued(p, u):
                    v.wait_ge(s_row[u], of_slot(p, u))
                    for j in range(2):
                        half = slice(j * C, (j + 1) * C)
                        last = v.tensor_scalar(ind[half, u, :], rowd[half, u, 1 + j * P:1 + (j + 1) * P],
                                               rowd[half, u, 0:1], None, ALU.is_equal)
                    last.then_inc(q.ind, 1)

                def message(p, u):
                    sh = t.edge_sh[:, bass.ds(p * 2, 2), :]
                    sh0 = sh[:, :, 0:1].broadcast_to((P, 2, C))
                    shx = sh[:, :, 1:4].unsqueeze(3).broadcast_to((P, 2, 3, C))
                    k = 12 * p if isinstance(p, int) else p * 12
                    v.wait_ge(q.up, p + 1)
                    if before(p):
                        v.wait_ge(q.msg, p)
                    v.tensor_tensor(xs0[:, :, :], p_up[:, :, 0, :], sh0, ALU.mult)
                    v.tensor_tensor(dx[:, :, :, :], p_up[:, :, 1:4, :], shx, ALU.mult)
                    v.wait_ge(q.tpw, p + 1)
                    v.tensor_tensor(pp[:, :, :], p_up[:, :, 0, :], tpw[:, :, 1, :], ALU.mult)
                    v.tensor_tensor(qq[:, :, :], tpw[:, :, 2, :], sh0, ALU.mult)
                    v.drain()
                    v.tensor_tensor(dot[:, :, :], dx[:, :, 0, :], dx[:, :, 1, :], ALU.add)
                    v.tensor_tensor(ma[:, :, :], tpw[:, :, 0, :], xs0[:, :, :], ALU.mult)
                    v.tensor_tensor(mp[:, :, :, :], pp[:, :, :].unsqueeze(2).broadcast_to((P, 2, 3, C)), shx, ALU.mult)
                    v.tensor_tensor(mq[:, :, :, :], p_up[:, :, 1:4, :],
                                    qq[:, :, :].unsqueeze(2).broadcast_to((P, 2, 3, C)), ALU.mult)
                    v.drain()
                    v.tensor_tensor(dot[:, :, :], dot[:, :, :], dx[:, :, 2, :], ALU.add)
                    if before(p, 2):
                        v.wait_ge(q.psum, p - 1)
                    v.tensor_tensor(msg[:, u, :, 1:4, :], mp[:, :, :, :], mq[:, :, :, :], ALU.add)
                    v.drain()
                    v.tensor_tensor(mb[:, :, :], tpw[:, :, 3, :], dot[:, :, :], ALU.mult).then_inc(q.m, 1)
                    v.drain()
                    v.tensor_tensor(msg[:, u, :, 0, :], ma[:, :, :], mb[:, :, :], ALU.add).then_inc(q.msg, 1)

                def carried(p, u):
                    v.wait_ge(q.psum, p + 1)
                    if before(p):
                        v.wait_ge(q.carry, p)
                        for x in range(4):
                            last = v.scalar_tensor_tensor(sumT[:, u, x, :], ind[:, u, :], p_carry[:, x:x + 1],
                                                          p_sum[:, x, :], ALU.mult, ALU.add)
                    else:
                        last = v.tensor_copy(sumT[:, u, :, :], p_sum[:, :, :])
                    last.then_inc(q.sum, 1)

                def basis(p, u):
                    A0, c4, w3, c0, w0, c2 = linT[:, 0, :], *(t.wc[:, k:k + 1] for k in (4, 5, 6, 7, 8))
                    v.wait_ge(q.lin, p + 1)
                    v.tensor_tensor(vv[:, :], sq[:, 0, :], sq[:, 1, :], ALU.add)
                    v.tensor_tensor(pb[:, :], aff[:, 0, :], A0, ALU.mult)
                    v.tensor_tensor(pg[:, :], aff[:, 1, :], A0, ALU.mult)
                    v.drain()
                    v.tensor_tensor(vv[:, :], vv[:, :], sq[:, 2, :], ALU.add)
                    v.drain()
                    v.scalar_tensor_tensor(pb[:, :], vv[:, :], c4, pb[:, :], ALU.mult, ALU.add)
                    v.scalar_tensor_tensor(pg[:, :], vv[:, :], w3, pg[:, :], ALU.mult, ALU.add)
                    v.drain()
                    v.scalar_tensor_tensor(pb[:, :], pb[:, :], c0, A0, ALU.add, ALU.mult)
                    if before(p, 2):
                        v.wait_ge(q.o, p - 1)
                    v.scalar_tensor_tensor(basT[:, u, 1:4, :], pg[:, :].unsqueeze(1).broadcast_to((P, 3, P)), w0,
                                           linT[:, 1:4, :], ALU.add, ALU.mult)
                    v.drain()
                    v.scalar_tensor_tensor(basT[:, u, 0, :], vv[:, :], c2, pb[:, :], ALU.mult, ALU.add)\
                        .then_inc(q.bas, 1)
                    v.drain()

                v.memset(hd[:, :, :, 0:1], 1.0)
                v.memset(lhid[:, :, :], 0.0).then_inc(q.clear, 1)
                staged(v, n, 2, [(1, continued), (1, message), (2, carried), (3, basis)])
                v.wait_ge(q.stat, n)
                v.tensor_tensor(t.gram[:, 0:1], t.gram[:, 0:1], p_stat[:, D:D + 1], ALU.subtract)
                v.tensor_tensor(t.gram[:, 1:1 + D], t.gram[:, 1:1 + D], p_stat[:, 0:D], ALU.subtract)
                v.tensor_copy(t.edge_sums[:, :], p_stat[0:1, D + 1:D + 1 + 3 * C])
                v.drain()


def norms(nc, t):
    nodes = float(t.nodes)
    with ExitStack() as ctx:
        def sb(name, shape, dt=f32):
            return ctx.enter_context(nc.sbuf_tensor(name, shape, dt))

        gm = sb("gm", [P, 2, P])
        va = sb("va", [P, 3, C])
        r = sb("r", [P, 3, C])
        mom = sb("mom", [P, 2, C])
        std = sb("nstd", [P, 2, C])
        inv = sb("ninv", [P, 2, C])
        cor = sb("ncor", [P, 2, C])
        m1 = sb("nm1", [P, 1])
        fm = sb("fm", [P, 2, D])
        fmean = sb("fmean", [P, 2])
        ta = ctx.enter_context(nc.psum_tensor("ta", [P, 512], f32))
        rows = ctx.enter_context(nc.psum_tensor("rows", [P, 512], f32))
        pf = ctx.enter_context(nc.psum_tensor("pf", [P, 2, D], f32))
        s_g, s_t, s_v, s_rows, s_var, s_sd, s_f, s_pf = (
            ctx.enter_context(nc.semaphore(x)) for x in
            ("s_g", "s_t", "s_v", "s_rows", "s_var", "s_sd", "s_f", "s_pf"))
        low, high, ones = (t.const[:, k:k + P] for k in (K_LOW, K_HIGH, K_ONES))

        with nc.Block() as block:
            @block.vector
            def _(v):
                v.memset(gm[:, :, :], 0.0)
                v.drain()
                for b in range(2):
                    for j in range(2):
                        part = slice(j * C, (j + 1) * C)
                        at = 1 + b * P + j * C
                        last = v.tensor_copy(gm[part, b, part], t.gram[part, at:at + C])
                last = v.tensor_scalar(va[:, 2, :], t.wstk[:, 0, :], t.gram[:, 0:1], None, ALU.mult)
                last.then_inc(s_g, 1)
                v.wait_ge(s_t, 1)
                v.tensor_tensor(va[:, 0:2, :], t.wstk[:, :, :], ta[:, 0:2 * C].rearrange("p (b c) -> p b c", b=2),
                                ALU.mult).then_inc(s_v, 1)
                v.wait_ge(s_rows, 1)
                v.tensor_scalar(r[:, 0, :], rows[:, 0:C], 1 / nodes, None, ALU.mult)
                v.tensor_scalar(r[:, 1, :], rows[:, C:2 * C], 1 / (3 * nodes), EPS, ALU.mult, ALU.add)
                v.tensor_scalar(r[:, 2, :], rows[:, 2 * C:3 * C], 1 / nodes, None, ALU.mult)
                v.drain()
                v.tensor_tensor(mom[:, 0, :], r[:, 2, :], r[:, 2, :], ALU.mult)
                v.drain()
                v.tensor_tensor(mom[:, 0, :], r[:, 0, :], mom[:, 0, :], ALU.subtract)
                v.drain()
                v.tensor_scalar(r[:, 0, :], mom[:, 0, :], 0.0, EPS, ALU.max, ALU.add)
                v.drain().then_inc(s_var, 1)
                v.wait_ge(s_sd, 1)
                v.reciprocal(inv[:, :, :], std[:, :, :])
                v.drain()
                v.tensor_tensor(cor[:, :, :], inv[:, :, :], r[:, 0:2, :], ALU.mult)
                v.drain()
                v.scalar_tensor_tensor(cor[:, :, :], cor[:, :, :], -0.5, inv[:, :, :], ALU.mult, ALU.mult)
                v.drain()
                v.scalar_tensor_tensor(inv[:, :, :], cor[:, :, :], 1.5, inv[:, :, :], ALU.add, ALU.mult)
                v.drain()
                v.tensor_tensor(t.scale[:, 0:C], inv[:, 0, :], t.gb[:, 0, :], ALU.mult)
                for x in range(3):
                    v.tensor_tensor(t.scale[:, (1 + x) * C:(2 + x) * C], inv[:, 1, :], t.gb[:, 2, :], ALU.mult)
                v.memset(t.shift[:, :], 0.0)
                v.memset(fm[:, :, :], 0.0)
                v.drain()
                v.tensor_tensor(mom[:, 1, :], r[:, 2, :], t.scale[:, 0:C], ALU.mult)
                for b in range(2):
                    v.tensor_tensor(fm[:, b, b * P:(b + 1) * P], t.bd[:, 2 + b, :], t.scale[:, b * P:(b + 1) * P],
                                    ALU.mult)
                v.drain()
                v.tensor_tensor(t.shift[:, 0:C], t.gb[:, 1, :], mom[:, 1, :], ALU.subtract)
                for b in range(2):
                    v.tensor_tensor(fm[:, b, b * P:(b + 1) * P], fm[:, b, b * P:(b + 1) * P],
                                    t.const[:, K_IDENT:K_IDENT + P], ALU.add)
                v.drain()
                v.reduce_sum(m1[:, :], t.shift[:, 0:C], axis=mybir.AxisListType.X)
                v.reduce_sum(fmean[:, :], fm[:, :, :], axis=mybir.AxisListType.X)
                v.drain()
                v.tensor_scalar(m1[:, :], m1[:, :], 1 / D, None, ALU.mult)
                v.tensor_scalar(fmean[:, :], fmean[:, :], 1 / D, None, ALU.mult)
                v.drain()
                v.tensor_scalar(t.shift_c[:, :], t.shift[:, :], m1[:, 0:1], None, ALU.subtract)
                for b in range(2):
                    last = v.tensor_scalar(fm[:, b, :], fm[:, b, :], fmean[:, b:b + 1], None, ALU.subtract)
                v.drain().then_inc(s_f, 1)
                v.wait_ge(s_pf, 1)
                v.tensor_copy(t.fold[:, :, :], pf[:, :, :])
                v.drain()

            @block.tensor
            def _(pe):
                pe.wait_ge(s_g, 1)
                for b in range(2):
                    last = nc.tensor.matmul(ta[:, b * C:(b + 1) * C], gm[:, b, :], t.wstk[:, b, :],
                                            start=True, stop=True)
                last.then_inc(s_t, 1)
                pe.wait_ge(s_v, 1)
                nc.tensor.matmul(rows[:, 0:3 * C], t.const[0:1, K_ONES:K_ONES + P], t.edge_sums[:, :],
                                 start=True, stop=False, skip_group_check=True)
                nc.tensor.matmul(rows[:, 0:C], low, va[:, 0, :], start=False, stop=False, skip_group_check=True)
                nc.tensor.matmul(rows[:, C:2 * C], high, va[:, 0, :], start=False, stop=False, skip_group_check=True)
                nc.tensor.matmul(rows[:, C:2 * C], ones, va[:, 1, :], start=False, stop=False, skip_group_check=True)
                nc.tensor.matmul(rows[:, 2 * C:3 * C], low, va[:, 2, :], start=False, stop=True,
                                 skip_group_check=True).then_inc(s_rows, 1)
                pe.wait_ge(s_f, 1)
                for lb in range(2):
                    for cb in range(2):
                        last = nc.tensor.matmul(pf[:, lb, :], t.mixT[:, cb, lb * P:(lb + 1) * P], fm[:, cb, :],
                                                start=cb == 0, stop=cb == 1)
                last.then_inc(s_pf, 1)

            @block.scalar
            def _(act):
                act.wait_ge(s_var, 1)
                nc.scalar.activation(std[:, :, :], r[:, 0:2, :], ACT.Sqrt).then_inc(s_sd, 1)


def node_outputs(nc, d, t):
    n = t.chunks
    SLOTS = 4
    rows = d.out.rearrange("(c i p) f -> c p i f", i=TILES, p=P)
    with ExitStack() as ctx:
        def sb(name, shape, dt=f32):
            return ctx.enter_context(nc.sbuf_tensor(name, shape, dt))

        def sem(name):
            return ctx.enter_context(nc.semaphore(name))

        xT = sb("xT2", [P, SLOTS, 2, CHUNK])
        z = sb("z", [P, SLOTS, TILES, D])
        res = sb("res", [P, SLOTS, TILES, D])
        squares = sb("squares2", [P, TILES, D])
        ss = sb("ss2", [P, SLOTS, TILES])
        std = sb("std2", [P, SLOTS, TILES])
        var = sb("var2", [P, SLOTS, TILES])
        inv = sb("inv2", [P, SLOTS, TILES])
        near = sb("near2", [P, SLOTS, TILES])
        corr = sb("corr2", [P, SLOTS, TILES])
        rstd = sb("rstd2", [P, SLOTS, TILES])
        zp = ctx.enter_context(nc.psum_tensor("zp", [P, SLOTS, TILES, D], f32))
        s_x = [sem(f"s2_x{i}") for i in range(SLOTS)]
        s_out = [sem(f"s2_out{i}") for i in range(SLOTS)]
        s_zp, s_z, s_ss, s_std, s_r, s_res = map(sem, ("s2_zp", "s2_z", "s2_ss", "s2_std", "s2_r", "s2_res"))

        with nc.Block() as block:
            @block.sync
            def _(sp):
                for c in range(SLOTS):
                    sp.dma_start(xT[:, c], d.xT[c]).then_inc(s_x[c], 16)

                def load(c, u):
                    sp.wait_ge(s_zp, c + 1)
                    sp.dma_start(xT[:, u], d.xT[c + SLOTS]).then_inc(s_x[u], 16)

                with sp.Fori(0, n // SLOTS - 1) as it:
                    for u in range(SLOTS):
                        load(it * SLOTS + u, u)

            @block.gpsimd
            def _(pool):
                def store(c, u):
                    pool.wait_ge(s_res, c + 1)
                    pool.dma_start(rows[c], res[:, u]).then_inc(s_out[u], 16)

                with pool.Fori(0, n // SLOTS) as it:
                    for u in range(SLOTS):
                        store(it * SLOTS + u, u)
                for u in range(SLOTS):
                    pool.wait_ge(s_out[u], n // SLOTS * 16)

            @block.tensor
            def _(pe):
                def products(c, u, rnd, warm=True):
                    pe.wait_ge(s_x[u], rnd * 16 + 16)
                    if warm:
                        pe.wait_ge(s_z, c - (SLOTS - 1))
                    for i in range(TILES):
                        for lb in range(2):
                            last = nc.tensor.matmul(zp[:, u, i, :], xT[:, u, lb, i * P:(i + 1) * P],
                                                    t.fold[:, lb, :], start=lb == 0, stop=lb == 1)
                    last.then_inc(s_zp, 1)

                for c in range(SLOTS):
                    products(c, c, 0, False)
                with pe.Fori(1, n // SLOTS) as it:
                    for u in range(SLOTS):
                        products(it * SLOTS + u, u, it)

            @block.scalar
            def _(act):
                def turn(c, u):
                    act.wait_ge(s_z, c + 1)
                    for i in range(TILES):
                        nc.scalar.activation(squares[:, i, :], z[:, u, i, :], ACT.Square,
                                             accum_out=ss[:, u, i:i + 1]).then_inc(s_ss, 1)
                    act.wait_ge(s_ss, c * TILES + TILES)
                    nc.scalar.activation(std[:, u, :], ss[:, u, :], ACT.Sqrt, scale=1 / D, bias=t.eps[:, 0:1])\
                        .then_inc(s_std, 1)

                with act.Fori(0, n // SLOTS) as it:
                    for u in range(SLOTS):
                        turn(it * SLOTS + u, u)

            @block.vector
            def _(v):
                def scaled(c, u):
                    v.wait_ge(s_zp, c + 1)
                    for i in range(TILES):
                        last = v.scalar_tensor_tensor(z[:, u, i, :], zp[:, u, i, :],
                                                      t.rstd1[:, bass.ds(c * TILES + i, 1)], t.shift_c[:, :],
                                                      ALU.mult, ALU.add)
                    last.then_inc(s_z, 1)

                def normed(c, u):
                    v.wait_ge(s_ss, c * TILES + TILES)
                    v.tensor_scalar(var[:, u, :], ss[:, u, :], 1 / D, EPS, ALU.mult, ALU.add).then_inc(s_r, 1)
                    v.wait_ge(s_std, c + 1)
                    v.reciprocal(inv[:, u, :], std[:, u, :]).then_inc(s_r, 1)
                    v.wait_ge(s_r, c * 5 + 2)
                    v.tensor_tensor(near[:, u, :], inv[:, u, :], var[:, u, :], ALU.mult).then_inc(s_r, 1)
                    v.wait_ge(s_r, c * 5 + 3)
                    v.scalar_tensor_tensor(corr[:, u, :], near[:, u, :], -0.5, inv[:, u, :], ALU.mult, ALU.mult)\
                        .then_inc(s_r, 1)
                    v.wait_ge(s_r, c * 5 + 4)
                    v.scalar_tensor_tensor(rstd[:, u, :], corr[:, u, :], 1.5, inv[:, u, :], ALU.add, ALU.mult)\
                        .then_inc(s_r, 1)
                    v.wait_ge(s_r, c * 5 + 5)
                    for i in range(TILES):
                        last = v.tensor_scalar(res[:, u, i, :], z[:, u, i, :], rstd[:, u, i:i + 1], None, ALU.mult)
                    last.then_inc(s_res, 1)

                scaled(0, 0)
                for c in range(SLOTS):
                    scaled(c + 1, (c + 1) % SLOTS)
                    normed(c, c)
                with v.Fori(1, n // SLOTS - 1) as it:
                    for u in range(SLOTS):
                        scaled(it * SLOTS + u + 1, (u + 1) % SLOTS)
                        v.wait_ge(s_out[u], it * 16)
                        normed(it * SLOTS + u, u)
                for c in range(n - SLOTS, n):
                    if c + 1 < n:
                        scaled(c + 1, (c + 1) % SLOTS)
                    v.wait_ge(s_out[c % SLOTS], (n // SLOTS - 1) * 16)
                    normed(c, c % SLOTS)


def receiver_outputs(nc, d, t):
    n = t.pairs
    SLOTS = 4
    with ExitStack() as ctx:
        def sb(name, shape, dt=f32):
            return ctx.enter_context(nc.sbuf_tensor(name, shape, dt))

        def sem(name):
            return ctx.enter_context(nc.semaphore(name))

        hd = sb("hd2", [P, SLOTS, 2, D])
        o = sb("o2", [P, SLOTS, 2, D])
        z = sb("z2", [P, SLOTS, 2, D])
        res = sb("res2", [P, SLOTS, 2, D])
        unused = sb("unused", [P, 2, 2, D])
        at = sb("at3", [P, SLOTS, 2], i32)
        total = sb("total", [P, SLOTS, 2])
        less_mean = sb("less_mean", [P, SLOTS, 2])
        ss = sb("ss3", [P, SLOTS, 2])
        std = sb("std3", [P, SLOTS, 2])
        inv = sb("inv3", [P, SLOTS, 2])
        s_in = [sem(f"s3_in{i}") for i in range(SLOTS)]
        s_put = [sem(f"s3_put{i}") for i in range(SLOTS)]
        s_read, s_z, s_total, s_mean, s_ss, s_std, s_inv, s_res, s_at, s_go = map(
            sem, ("s3_read", "s3_z", "s3_total", "s3_mean", "s3_ss", "s3_std", "s3_inv", "s3_res", "s3_at", "s3_go"))
        scale = t.scale[:, :].unsqueeze(1).broadcast_to((P, 2, D))
        shift = t.shift[:, 0:C].unsqueeze(1).broadcast_to((P, 2, C))

        with nc.Block() as block:
            @block.sync
            def _(sp):
                def load(p, u):
                    if before(p, SLOTS):
                        sp.wait_ge(s_read, p - (SLOTS - 1))
                    sp.dma_start(hd[:, u], d.hd[p]).then_inc(s_in[u], 16)
                    sp.dma_start(o[:, u], d.o[p]).then_inc(s_in[u], 16)

                staged(sp, n, SLOTS, [(0, load)])

            @block.gpsimd
            def _(pool):
                bound = pool.to_reg(t.chunks * CHUNK - 1)

                def put(p, u):
                    pool.wait_ge(s_res, p + 1)
                    pool.tensor_copy(at[:, u, :], t.put[:, bass.ds(p * 2, 2)]).then_inc(s_at, 1)
                    pool.wait_ge(s_at, p + 1)
                    pool.sem_inc(s_go, 1)
                    for j in range(2):
                        pool.indirect_dma_start(
                            d.out, bass.IndirectOffsetOnAxis(ap=at[:, u, j:j + 1], axis=0),
                            res[:, u, j, :], None, bounds_check=bound,
                            oob_is_err=False).then_inc(s_put[u], 16)

                staged(pool, n, SLOTS, [(0, put)])
                for u in range(SLOTS):
                    pool.wait_ge(s_put[u], (n + SLOTS - 1 - u) // SLOTS * 32)

            @block.scalar
            def _(act):
                def sums(p, u):
                    act.wait_ge(s_z, p + 1)
                    if before(p):
                        act.wait_ge(s_total, 2 * p)
                    for j in range(2):
                        nc.scalar.activation(unused[:, 0, j, :], z[:, u, j, :], ACT.Copy,
                                             accum_out=total[:, u, j:j + 1]).then_inc(s_total, 1)

                def squares(p, u):
                    act.wait_ge(s_mean, p + 1)
                    if before(p):
                        act.wait_ge(s_ss, 2 * p)
                    for j in range(2):
                        nc.scalar.activation(unused[:, 1, j, :], z[:, u, j, :], ACT.Square,
                                             bias=less_mean[:, u, j:j + 1],
                                             accum_out=ss[:, u, j:j + 1]).then_inc(s_ss, 1)

                def root(p, u):
                    act.wait_ge(s_ss, 2 * p + 2)
                    nc.scalar.activation(std[:, u, :], ss[:, u, :], ACT.Sqrt, scale=1 / D, bias=t.eps[:, 0:1])\
                        .then_inc(s_std, 1)

                staged(act, n, SLOTS, [(2, root), (1, squares), (0, sums)])

            @block.vector
            def _(v):
                def summed(p, u):
                    v.wait_ge(s_in[u], of_slot(p, u, 32, SLOTS))
                    v.tensor_tensor(z[:, u], o[:, u], scale, ALU.mult)
                    v.drain()
                    v.tensor_tensor(z[:, u], z[:, u], hd[:, u], ALU.add).then_inc(s_read, 1)

                def shifted(p, u):
                    v.wait_ge(s_read, p + 1)
                    v.tensor_tensor(z[:, u, :, 0:C], z[:, u, :, 0:C], shift, ALU.add).then_inc(s_z, 1)

                def mean(p, u):
                    v.wait_ge(s_total, 2 * p + 2)
                    v.tensor_scalar(less_mean[:, u, :], total[:, u, :], -1 / D, None, ALU.mult).then_inc(s_mean, 1)

                def inverse(p, u):
                    v.wait_ge(s_std, p + 1)
                    v.reciprocal(inv[:, u, :], std[:, u, :]).then_inc(s_inv, 1)

                def normed(p, u):
                    if before(p, SLOTS):
                        v.wait_ge(s_put[u], of_slot(p - SLOTS, u, 32, SLOTS))
                    v.wait_ge(s_inv, p + 1)
                    for j in range(2):
                        last = v.tensor_scalar(res[:, u, j, :], z[:, u, j, :], less_mean[:, u, j:j + 1],
                                               inv[:, u, j:j + 1], ALU.add, ALU.mult)
                    last.then_inc(s_res, 1)

                staged(v, n, SLOTS, [(3, inverse), (1, mean), (0, summed), (3, normed), (0, shifted)])


def build(nc, d, shapes, phases=None):
    with ExitStack() as ctx:
        t = tensors(nc, ctx, shapes)
        prepare(nc, d, t)
        rotate(nc, d, t)
        mix_matrix(nc, t)
        node_stats(nc, d, t)
        edges(nc, d, t)
        norms(nc, t)
        node_outputs(nc, d, t)
        receiver_outputs(nc, d, t)


def arrays_of(inputs):
    x = np.asarray(inputs["x"])
    src, dst = np.asarray(inputs["src"]), np.asarray(inputs["dst"])
    nodes, n_edges = x.shape[0], src.shape[0]
    chunks = -(-(nodes + 1) // (CHUNK * 4)) * 4
    pairs = -(-n_edges // (PAIR * 2)) * 2
    e = pairs * PAIR
    xp = np.zeros((chunks * CHUNK, D), np.float32)
    xp[:nodes] = x
    srcp, dstp = np.full(e, nodes, np.int32), np.full(e, nodes, np.int32)
    srcp[:n_edges], dstp[:n_edges] = src, dst
    nxt = np.full(e, nodes + 1, np.int32)
    nxt[:-1] = dstp[1:]
    row = np.full(e + 1, nodes + 1, np.int32)
    row[1:] = dstp
    angle = np.zeros(e, np.float32)
    angle[:n_edges] = np.asarray(inputs["edge_weight"])
    rbf = np.zeros((e, 16), np.float32)
    rbf[:n_edges] = np.asarray(inputs["edge_attr_16"])
    sh = np.zeros((e, 4), np.float32)
    sh[:n_edges] = np.asarray(inputs["edge_attr_4"])
    cols = lambda a: a.reshape((2 * pairs, P) + a.shape[1:]).swapaxes(0, 1)
    w = {k[len("L1_gnn_"):]: np.asarray(v) for k, v in inputs.items() if k.startswith("L1_gnn_")}

    def blocks(a, b):
        out = np.zeros((a.shape[0] + b.shape[0], a.shape[1] + b.shape[1]), np.float32)
        out[:a.shape[0], :a.shape[1]] = a
        out[a.shape[0]:, a.shape[1]:] = b
        return out

    bd = np.stack([blocks(w["W_up0"], w["W_up1"]), blocks(w["W_up1"], w["W_up1"]),
                   blocks(w["Wsc0"], w["Wsc1"]), blocks(w["Wsc1"], w["Wsc1"]),
                   blocks(w["W_lin0"], w["W_lin0"]), blocks(w["W_lin1"], w["W_lin1"]),
                   blocks(w["WB0"], w["WB0"]), blocks(w["WB1"], w["WB1"])], 1)
    twice = lambda a: np.concatenate([a, a], 0)
    c, g = w["Wc0"], w["Wc1"]
    wc = twice(np.stack([c[:, 3], g[:, 2], c[:, 1], g[:, 1], c[:, 4], g[:, 3], c[:, 0], g[:, 0], c[:, 2]], 1))
    k = np.zeros((P, K_ALL), np.float32)
    part, low = np.arange(P), np.arange(P) < C
    k[:, K_IDENT:K_IDENT + P] = np.eye(P)
    k[:, K_DUP:K_DUP + P] = (part[:, None] == C + part[None, :] % C)
    k[:, K_LOW:K_LOW + P] = low[:, None]
    k[:, K_HIGH:K_HIGH + P] = ~low[:, None]
    k[:, K_ONES:K_ONES + P] = 1
    k[:, K_TRI:K_TRI + P] = part[:, None] < part[None, :]
    k[:, K_EYE2:K_EYE2 + C] = part[:, None] % C == np.arange(C)[None, :]
    source = np.concatenate([np.arange(C)] + [C + 3 * np.arange(C) + a for a in range(3)])
    for lb in range(2):
        k[:, K_PLANES + lb * D:K_PLANES + (lb + 1) * D] = (lb * P + part)[:, None] == source[None, :]
    k[P - 1, K_ROW127:K_ROW127 + P] = 1
    k[:, K_ROW:K_ROW + 2] = part[:, None] + P * np.arange(2)
    k[:, K_DOWN:K_DOWN + STEPS + 1] = STEPS + 1 - np.arange(STEPS + 1)
    arrays = {
        "xT": xp.reshape(chunks, CHUNK, 2, P).transpose(0, 3, 2, 1),
        "steps": np.stack([srcp.reshape(P, -1), dstp.reshape(P, -1), angle.view(np.int32).reshape(P, -1)], 1),
        "rbf": rbf.reshape(pairs, 2, P, 16).transpose(0, 1, 3, 2).reshape(pairs, 32, P),
        "edge_idx": np.stack([cols(srcp), cols(dstp), cols(nxt)], 1),
        "edge_sh": cols(sh),
        "dst_row": row,
        "const": k,
        "bd": bd,
        "m1": blocks(w["M1"], w["M1"]),
        "m23": np.stack([blocks(w["M2"], w["M2"]), blocks(w["M3"], w["M3"])], 1),
        "m4": twice(w["M4"]),
        "wstk": np.stack([np.concatenate([w["Wsc0"], w["Wsc1"]], 0), twice(w["Wsc1"])], 1),
        "wc": wc,
        "gb": np.stack([w["gamma0"], w["beta0"], w["gamma1"]], 0),
    }
    arrays = {n: np.ascontiguousarray(a) for n, a in arrays.items()}
    return arrays, {"nodes": nodes, "chunks": chunks, "pairs": pairs}


def declare(nc, arrays, shapes):
    def given(name):
        a = arrays[name]
        return nc.dram_tensor(f"in_{name}", a.shape, mybir.dt.from_np(a.dtype), kind="ExternalInput").ap()

    d = Named()
    d.xT, d.steps, d.rbf, d.const = given("xT"), given("steps"), given("rbf"), given("const")
    d.edge_idx, d.edge_sh, d.dst_row = given("edge_idx"), given("edge_sh"), given("dst_row")
    d.bd, d.m1, d.m23, d.m4 = given("bd"), given("m1"), given("m23"), given("m4")
    d.wstk, d.wc, d.gb = given("wstk"), given("wc"), given("gb")
    n, e = shapes["chunks"] * CHUNK, shapes["pairs"] * PAIR
    d.out = nc.dram_tensor("out", (n, D), f32, kind="ExternalOutput").ap()
    d.h = nc.dram_tensor("h_scratch", (n, D), f32, kind="Internal").ap()
    d.hd = nc.dram_tensor("hd_scratch", (shapes["pairs"], P, 2, D), f32, kind="Internal").ap()
    d.o = nc.dram_tensor("o_scratch", (shapes["pairs"], P, 2, D), f32, kind="Internal").ap()
    d.recs = nc.dram_tensor("recs_scratch", (e, REC), f32, kind="Internal").ap()
    d.n_sets = nc.dram_tensor("sets_scratch", (1, 1), i32, kind="Internal").ap()
    return d


def kernel(**inputs):
    import concourse.bacc as bacc
    from concourse.bass_utils import run_bass_kernel_spmd

    arrays, shapes = arrays_of(inputs)
    nc = bacc.Bacc("TRN2", target_bir_lowering=False, num_devices=1)
    d = declare(nc, arrays, shapes)
    build(nc, d, shapes)
    got = run_bass_kernel_spmd(nc, [{f"in_{n}": a for n, a in arrays.items()}], core_ids=[0])
    planes = got.results[0]["out"][:shapes["nodes"]].reshape(-1, 4, C)
    return np.concatenate([planes[:, 0], planes[:, 1:].swapaxes(1, 2).reshape(-1, 3 * C)], 1)
```

```python
from contextlib import ExitStack

import numpy as np

import concourse.bass as bass
import concourse.mybir as mybir

f32 = mybir.dt.float32
bf16 = mybir.dt.bfloat16
f32r = mybir.dt.float32r
i32 = mybir.dt.int32
ALU = mybir.AluOpType
ACT = mybir.ActivationFunctionType

P = 128
D = 256
C = 64
TILES = 4
CHUNK = P * TILES
PAIR = 2 * P
FIELDS = 8
STEPS = 512
OUT = D
EPS = 1e-5
SKIP = 1 << 20
TWO_PI = 2 * np.pi
TWO_PI_HI = 6.28125
TWO_PI_LO = TWO_PI - TWO_PI_HI
ROUND = 1.5 * 2.0 ** 23
BELOW_PI = 3.1415925

K_IDENT, K_DUP, K_LOW, K_HIGH, K_ONES, K_TRI, K_PLANES = (k * P for k in range(7))
K_ROW127 = K_PLANES + 2 * D
K_ROW = K_ROW127 + P
K_DOWN = K_ROW + 2
K_IOTA = K_DOWN + STEPS + 1
K_SPREAD = K_IOTA + 2 * P
K_ALL = K_SPREAD + 4 * P


class Named:
    pass


def tensors(nc, ctx, shapes):
    n_chunks, n_pairs = shapes["chunks"], shapes["pairs"]

    def sb(name, shape, dt=f32):
        return ctx.enter_context(nc.sbuf_tensor(name, shape, dt))

    t = Named()
    t.chunks, t.pairs, t.nodes = n_chunks, n_pairs, shapes["nodes"]
    t.const = sb("const", [P, K_ALL])
    t.matT = sb("matT", [P, 2, D])
    t.mix = sb("mix", [P, 2, D])
    t.mixT = sb("mixT", [P, 2, D])
    t.mix_high = sb("mix_high", [P, 2, D], f32r)
    t.mix_low = sb("mix_low", [P, 2, D], f32r)
    t.rstd1 = sb("rstd1", [P, n_chunks * TILES])
    t.gram = sb("gram", [P, 1 + 2 * P])
    t.edge_sums = sb("edge_sums", [1, 3 * C])
    t.scale = sb("scale", [P, D])
    t.shift = sb("shift", [P, D])
    t.shift_c = sb("shift_c", [P, D])
    t.fold = sb("fold", [P, 2, D])
    t.fold_high = sb("fold_high", [P, 2, D], f32r)
    t.fold_low = sb("fold_low", [P, 2, D], f32r)
    t.eps = sb("eps", [P, 1])
    t.n_sets = sb("n_sets", [P, 1], i32)
    t.hidden = sb("hidden", [P, n_pairs, P])
    t.bd = sb("bd", [P, 8, P])
    t.m1 = sb("m1", [32, P])
    t.m23 = sb("m23", [P, 2, P])
    t.m4 = sb("m4", [P, D])
    t.wstk = sb("wstk", [P, 2, C])
    t.wc = sb("wc", [P, 9])
    t.gb = sb("gb", [P, 3, C])
    t.edge_idx = sb("edge_idx", [P, 3, 2 * n_pairs], i32)
    t.edge_sh = sb("edge_sh", [P, 2 * n_pairs, 4])
    t.edge_sh0 = sb("edge_sh0", [P, 2 * n_pairs])
    t.dstf = sb("dstf", [P, 2 * n_pairs])
    t.last = sb("last", [P, 2 * n_pairs])
    t.put = sb("put", [P, 2 * n_pairs], i32)
    return t


def staged(eng, n, unroll, stages):
    lags = [lag for lag, _ in stages]
    low, high = min(min(lags), 0), max(lags)

    first = -(-(high + unroll) // unroll) * unroll
    end = (n + low) // unroll * unroll

    def turn(p, u):
        for lag, stage in stages:
            if not isinstance(p, int) or 0 <= p - lag < n:
                stage(p - lag, (u - lag) % unroll)

    for p in range(low, min(first, end)):
        turn(p, p % unroll)
    if end > first:
        with eng.Fori(first // unroll, end // unroll) as it:
            for u in range(unroll):
                turn(it * unroll + u, u)
    for p in range(end, n + high):
        turn(p, p % unroll)


def before(p, k=1):
    return not isinstance(p, int) or p >= k


def of_slot(p, u, per=16, unroll=2):
    return (p // unroll + 1) * per if isinstance(p, int) else (p - u) * (per // unroll) + per


def prepare(nc, d, t, packed):
    n_pairs = t.pairs
    COLS = 2 * n_pairs
    batches = n_pairs // 2
    with ExitStack() as ctx:
        def sb(name, shape, dt=f32):
            return ctx.enter_context(nc.sbuf_tensor(name, shape, dt))

        def ps(name, shape):
            return ctx.enter_context(nc.psum_tensor(name, shape, f32))

        def sem(name):
            return ctx.enter_context(nc.semaphore(name))

        steps = sb("steps", [P, 3, COLS], i32)
        fij = sb("fij", [P, 2, COLS])
        inr = sb("inr", [P, 2, COLS])
        turns = sb("turns", [P, COLS])
        ang = sb("ang", [P, COLS])
        mag = sb("mag", [P, COLS])
        trig = sb("trig", [P, 2, COLS])
        more = sb("more", [P, 2, COLS])
        least = sb("least", [P, 2, COLS])
        active = sb("active", [P, COLS])
        zeros = sb("zeros", [P, COLS])
        counts = sb("counts", [P, 2, COLS])
        run = sb("run", [P, COLS])
        base = sb("base", [P, COLS], i32)
        place = sb("place", [P, COLS])
        cnt = sb("cnt", [P, 1])
        half_pi = sb("half_pi", [P, 1])
        iota = sb("iota", [P, 2 * P], bf16)
        fields = sb("fields", [P, COLS, FIELDS], bf16)
        moved = sb("moved", [P, 2, 4, FIELDS], bf16)
        onehot = sb("onehot", [P, 2, 4, 2 * P], bf16)
        rbf = sb("rbf", [32, 2, 2 * P])
        hid1 = sb("hid1", [P, 2, 2 * P])
        hid2 = sb("hid2", [P, 2, 2 * P])
        p_counts = ps("p_counts", [P, 512])
        window = ps("window", [FIELDS, 2, 2, 2 * P])
        net = [ps(f"net{i}", [P, 512]) for i in range(3)]

        s_rbf = [sem("s_rbf0"), sem("s_rbf1")]
        s_net = [sem(f"s_net{i}") for i in range(3)]
        s_silu = [sem(f"s_silu{i}") for i in range(3)]
        (s_const, s_steps, s_weights, s_edge, s_active, s_angle, s_trig, s_half, s_counts, s_fields, s_moved,
         s_onehot, s_window, s_packed, s_base, s_go) = map(
            sem, ("s_const", "s_steps", "s_weights", "s_edge", "s_active", "s_angle", "s_trig", "s_half",
                  "s_counts", "s_fields", "s_moved", "s_onehot", "s_window", "s_packed", "s_base", "s_go_prepare"))

        with nc.Block() as block:
            @block.sync
            def _(sp):
                sp.dma_start(steps[:, :, :], d.steps).then_inc(s_steps, 16)
                sp.dma_start(t.const[:, :], d.const).then_inc(s_const, 16)
                sp.dma_start(t.m1[:, :], d.m1).then_inc(s_weights, 16)
                sp.dma_start(t.m23[:, :, :], d.m23).then_inc(s_weights, 16)

                def load(b, u):
                    if before(b, 2):
                        sp.wait_ge(s_net[0], b - 1)
                    sp.dma_start(rbf[:, u, :], d.rbf[b]).then_inc(s_rbf[u], 16)

                staged(sp, batches, 2, [(0, load)])
                sp.dma_start(t.bd[:, :, :], d.bd).then_inc(s_edge, 16)
                sp.dma_start(t.m4[:, :], d.m4).then_inc(s_edge, 16)
                sp.dma_start(t.wstk[:, :, :], d.wstk).then_inc(s_edge, 16)
                sp.dma_start(t.wc[:, :], d.wc).then_inc(s_edge, 16)
                sp.dma_start(t.gb[:, :, :], d.gb.partition_broadcast(P)).then_inc(s_edge, 16)
                sp.dma_start(t.edge_idx[:, :, :], d.edge_idx).then_inc(s_edge, 16)
                sp.dma_start(t.edge_sh[:, :, :], d.edge_sh).then_inc(s_edge, 16)

            @block.tensor
            def _(pe):
                def layer1(b, u):
                    pe.wait_ge(s_rbf[u], of_slot(b, u))
                    if before(b):
                        pe.wait_ge(s_silu[0], b)
                    nc.tensor.matmul(net[0][:, 0:2 * P], t.m1[:, :], rbf[:, u, :], start=True, stop=True)\
                        .then_inc(s_net[0], 1)

                def layer2(b, u):
                    pe.wait_ge(s_silu[0], b + 1)
                    if before(b):
                        pe.wait_ge(s_silu[1], b)
                    nc.tensor.matmul(net[1][:, 0:2 * P], t.m23[:, 0, :], hid1[:, u, :], start=True, stop=True)\
                        .then_inc(s_net[1], 1)

                def layer3(b, u):
                    pe.wait_ge(s_silu[1], b + 1)
                    if before(b):
                        pe.wait_ge(s_silu[2], b)
                    nc.tensor.matmul(net[2][:, 0:2 * P], t.m23[:, 1, :], hid2[:, u, :], start=True, stop=True)\
                        .then_inc(s_net[2], 1)

                def pack(b, u):
                    pe.wait_ge(s_onehot, b + 1)
                    pe.wait_ge(s_moved, b + 1)
                    if before(b, 2):
                        pe.wait_ge(s_packed, 2 * b - 2)
                    for g in range(2):
                        for c in range(2):
                            last = nc.tensor.matmul(window[:, u, g, :], moved[:, u, 2 * g + c, :],
                                                    onehot[:, u, 2 * g + c, :], start=c == 0, stop=c == 1)
                    last.then_inc(s_window, 1)

                pe.wait_ge(s_const, 16)
                pe.wait_ge(s_active, 1)
                nc.tensor.matmul(p_counts[:, 0:COLS], t.const[:, K_TRI:K_TRI + P], active[:, :],
                                 start=True, stop=True)
                nc.tensor.matmul(p_counts[:, COLS:2 * COLS], t.const[:, K_ONES:K_ONES + P], active[:, :],
                                 start=True, stop=True).then_inc(s_counts, 1)
                pe.wait_ge(s_weights, 32)
                staged(pe, batches, 2, [(2, layer3), (1, layer2), (0, layer1), (1, pack)])

            @block.scalar
            def _(act):
                def silu(k, out):
                    def stage(b, u):
                        act.wait_ge(s_net[k], b + 1)
                        nc.scalar.activation(out(b, u), net[k][:, 0:2 * P], ACT.Silu).then_inc(s_silu[k], 1)
                    return stage

                def append(b, u):
                    at = act.value_load(base[0:1, bass.ds(b * 4 + 2, 1)], min_val=0, max_val=P * COLS)
                    act.wait_ge(s_packed, 2 * b + 1)
                    nc.scalar.activation(packed[:, bass.ds(at, 2 * P)], window[:, u, 1, :], ACT.Copy)\
                        .then_inc(s_packed, 1)

                act.wait_ge(s_half, 1)
                act.wait_ge(s_angle, 1)
                nc.scalar.activation(trig[:, 1, :], ang[:, :], ACT.Sin).then_inc(s_trig, 1)
                nc.scalar.activation(trig[:, 0, :], mag[:, :], ACT.Sin, scale=-1.0, bias=half_pi[:, 0:1])\
                    .then_inc(s_trig, 1)
                act.wait_ge(s_base, 1)
                act.sem_inc(s_go, 1)
                staged(act, batches, 2, [(3, append),
                    (2, silu(2, lambda b, u: t.hidden[:, bass.ds(b * 2, 2), :])),
                    (1, silu(1, lambda b, u: hid2[:, u, :])),
                    (0, silu(0, lambda b, u: hid1[:, u, :]))])

            @block.vector
            def _(v):
                v.memset(half_pi[:, :], np.pi / 2).then_inc(s_half, 1)
                v.memset(t.eps[:, :], EPS)
                v.memset(zeros[:, :], 0.0)
                v.memset(packed[:, :], 0.0)
                v.wait_ge(s_steps, 16)
                v.tensor_copy(fij[:, :, :], steps[:, 0:2, :])
                v.tensor_scalar(turns[:, :], steps[:, 2, :].bitcast(f32), 1 / TWO_PI, ROUND, ALU.mult, ALU.add)
                v.drain()
                v.tensor_scalar(inr[:, :, :], fij[:, :, :], float(D), None, ALU.is_lt)
                v.tensor_scalar(turns[:, :], turns[:, :], ROUND, None, ALU.subtract)
                v.drain()
                v.tensor_tensor(active[:, :], inr[:, 0, :], inr[:, 1, :], ALU.max).then_inc(s_active, 1)
                v.scalar_tensor_tensor(ang[:, :], turns[:, :], -TWO_PI_HI, steps[:, 2, :].bitcast(f32),
                                       ALU.mult, ALU.add)
                v.drain()
                v.scalar_tensor_tensor(ang[:, :], turns[:, :], -TWO_PI_LO, ang[:, :], ALU.mult, ALU.add)
                v.drain()
                v.tensor_scalar(ang[:, :], ang[:, :], BELOW_PI, -BELOW_PI, ALU.min, ALU.max)
                v.drain()
                v.scalar_tensor_tensor(mag[:, :], ang[:, :], -1.0, ang[:, :], ALU.mult, ALU.max)\
                    .then_inc(s_angle, 1)
                v.tensor_scalar(fields[:, :, 0:2].rearrange("p c w -> p w c"), fij[:, :, :], float(OUT), -float(OUT),
                                ALU.min, ALU.add)
                v.wait_ge(s_const, 16)
                v.tensor_copy(iota[:, :], t.const[:, K_IOTA:K_IOTA + 2 * P])
                v.wait_ge(s_counts, 1)
                v.tensor_copy(counts[:, :, :], p_counts[:, 0:2 * COLS].rearrange("p (k c) -> p k c", k=2))
                v.drain()
                v.tensor_tensor_scan(run[:, :], counts[:, 1, :], zeros[:, :], 0.0, ALU.add, ALU.add)
                v.tensor_tensor(counts[:, 0, 1::2], counts[:, 0, 1::2], counts[:, 1, 0::2], ALU.add)
                v.drain()
                v.tensor_tensor(base[:, :], run[:, :], counts[:, 1, :], ALU.subtract)
                v.tensor_scalar(cnt[:, :], run[:, COLS - 1:COLS], 1 / STEPS, 0.5 - 1 / (4 * STEPS), ALU.mult, ALU.add)
                v.scalar_tensor_tensor(place[:, :], active[:, :], float(4 * P), counts[:, 0, :], ALU.mult, ALU.add)
                v.drain()
                v.tensor_scalar(cnt[:, :], cnt[:, :], ROUND, None, ALU.add)
                v.tensor_scalar(place[:, :], place[:, :], float(4 * P), None, ALU.subtract)
                v.drain()
                v.tensor_scalar(t.n_sets[:, :], cnt[:, :], ROUND, 1.0, ALU.subtract, ALU.max).then_inc(s_base, 1)
                part = [fields[:, :, 2 + k:8:3].rearrange("p c w -> p w c") for k in range(3)]
                v.wait_ge(s_trig, 2)
                v.tensor_copy(part[0], trig[:, :, :])
                v.drain()
                v.tensor_tensor(more[:, :, :], trig[:, :, :], part[0], ALU.subtract)
                v.drain()
                v.tensor_copy(part[1], more[:, :, :])
                v.drain()
                v.tensor_tensor(least[:, :, :], more[:, :, :], part[1], ALU.subtract)
                v.drain()
                v.tensor_copy(part[2], least[:, :, :]).then_inc(s_fields, 1)
                v.drain()

                def places(b, u):
                    if before(b, 2):
                        v.wait_ge(s_window, b - 1)
                    for c in range(4):
                        last = v.tensor_scalar(onehot[:, u, c, :], iota[:, :], place[:, bass.ds(b * 4 + c, 1)], None,
                                               ALU.is_equal)
                    last.then_inc(s_onehot, 1)

                def append(b, u):
                    at = v.value_load(base[0:1, bass.ds(b * 4, 1)], min_val=0, max_val=P * COLS)
                    v.wait_ge(s_window, b + 1)
                    if before(b):
                        v.wait_ge(s_packed, 2 * b)
                    v.tensor_copy(packed[:, bass.ds(at, 2 * P)], window[:, u, 0, :]).then_inc(s_packed, 1)

                staged(v, batches, 2, [(0, places), (2, append)])
                v.wait_ge(s_edge, 112)
                v.tensor_copy(t.dstf[:, :], t.edge_idx[:, 1, :])
                v.tensor_copy(t.edge_sh0[:, :], t.edge_sh[:, :, 0])
                v.tensor_tensor(t.last[:, :], t.edge_idx[:, 1, :], t.edge_idx[:, 2, :], ALU.not_equal)
                v.tensor_scalar(t.m4[:, 3 * C:4 * C], t.m4[:, 3 * C:4 * C], float(1 / np.sqrt(3.0)), None, ALU.mult)
                v.drain()
                v.tensor_scalar(run[:, :], t.last[:, :], -float(SKIP), float(SKIP), ALU.mult, ALU.add)
                v.drain()
                v.tensor_tensor(t.put[:, :], run[:, :], t.dstf[:, :], ALU.add)
                v.drain()

            @block.gpsimd
            def _(pool):
                def move(b, u):
                    if before(b, 2):
                        pool.wait_ge(s_window, b - 1)
                    pool.tensor_copy(moved[:, u, :, :], fields[:, bass.ds(b * 4, 4), :]).then_inc(s_moved, 1)

                pool.wait_ge(s_fields, 1)
                staged(pool, batches, 2, [(0, move)])


def rotate(nc, t, packed):
    with ExitStack() as ctx:
        def sb(name, shape, dt=f32):
            return ctx.enter_context(nc.sbuf_tensor(name, shape, dt))

        def sem(name):
            return ctx.enter_context(nc.semaphore(name))

        ops = sb("ops", [P, 4, STEPS + 1])
        spread = sb("spread", [FIELDS, 4, P], bf16)
        wide = sb("wide", [P, 3, STEPS + 1])
        plain = sb("plain", [P, STEPS])
        trig = sb("plain_trig", [P, 2, STEPS])
        hit = sb("hit", [P, 2, STEPS])
        signed = sb("signed", [P, 2, STEPS])
        coef = sb("coef", [P, 2, STEPS])
        kept = sb("kept", [P, 2, STEPS])
        add = sb("add", [P, 2, STEPS])
        pmap = sb("pmap", [P, 2, STEPS + 1])
        qmap = sb("qmap", [P, 2, STEPS + 1])
        left = sb("left", [P, STEPS + 1])
        first = sb("first", [P, 1])
        at = sb("at_end", [P, 1], i32)
        ends = sb("ends", [P, 2])
        ends_i = sb("ends_i", [P, 2], i32)
        is_ij = sb("is_ij", [P, 2, 2])
        pick = sb("pick", [P, 2, 2, P])
        coming = sb("coming", [P, 5, 2])
        now = sb("now", [P, 5, 2])
        part = sb("part", [P, 2, 2])
        clamped = sb("clamped_at", [P, 2])
        read = sb("read", [P, 2, 2])
        only_i = sb("only_i", [P, 2])
        written = sb("written", [P, 2])
        rest = sb("rest", [P, 2, D])
        mat = sb("mat", [P, 2, D])
        p_ops = ctx.enter_context(nc.psum_tensor("p_ops", [P, 4, STEPS], f32))
        row255 = ctx.enter_context(nc.psum_tensor("row255", [P, 512], f32))
        rows_ij = ctx.enter_context(nc.psum_tensor("rows_ij", [P, 2, D], f32))
        tp = ctx.enter_context(nc.psum_tensor("tp_mat", [P, 2, D], f32))
        s_spread, s_ops, s_loaded, s_used, s_ends, s_mat, s_255, s_mapped, s_ij, s_done, s_tp, s_go = map(
            sem, ("s_spread", "s_ops", "s_loaded", "s_used", "s_ends", "s_mat", "s_255", "s_mapped", "s_ij",
                  "s_mat_done", "s_tp_mat", "s_go_set"))
        max_sets = t.pairs * PAIR // STEPS

        with nc.Block() as block:
            @block.scalar
            def _(act):
                n = act.value_load(t.n_sets[0:1, 0:1], min_val=1, max_val=max_sets)
                with act.Fori(0, n) as s:
                    act.wait_ge(s_ops, s + 1)
                    act.wait_ge(s_used, s + 1)
                    for k in range(4):
                        last = nc.scalar.activation(ops[:, k, 0:STEPS], p_ops[:, k, :], ACT.Copy,
                                                    bias=float(OUT) if k < 2 else 0.0)
                    last.then_inc(s_loaded, 1)

            @block.tensor
            def _(pe):
                pe.wait_ge(s_spread, 1)
                n = pe.value_load(t.n_sets[0:1, 0:1], min_val=1, max_val=max_sets)

                def spread_set(s):
                    for k in range(4):
                        last = nc.tensor.matmul(p_ops[:, k, :], spread[:, k, :], packed[:, bass.ds(s * STEPS, STEPS)],
                                                start=True, stop=True)
                    last.then_inc(s_ops, 1)

                with pe.Fori(0, n) as s:
                    spread_set(s)
                    pe.wait_ge(s_ends, s + 1)
                    pe.sem_inc(s_go, 1)
                    g0 = pe.value_load(ends_i[0:1, 0:1], min_val=0, max_val=t.pairs * PAIR + max_sets)
                    g1 = pe.value_load(ends_i[0:1, 1:2], min_val=0, max_val=t.pairs * PAIR + max_sets)
                    with pe.Fori(g0, g1) as g:
                        pe.wait_ge(s_mat, g + 1)
                        nc.tensor.matmul(row255[:, 0:D], t.const[:, K_ROW127:K_ROW127 + P], mat[:, 1, :],
                                         start=True, stop=True).then_inc(s_255, 1)
                        pe.wait_ge(s_mapped, g + 1)
                        for ij in range(2):
                            for b in range(2):
                                last = nc.tensor.matmul(rows_ij[:, ij, :], pick[:, ij, b, :], mat[:, b, :],
                                                        start=b == 0, stop=b == 1)
                        last.then_inc(s_ij, 1)
                pe.wait_ge(s_done, 1)
                for lb in range(2):
                    for kb in range(2):
                        last = nc.tensor.transpose(tp[:, lb, kb * P:(kb + 1) * P], mat[:, kb, lb * P:(lb + 1) * P],
                                                   t.const[:, K_IDENT:K_IDENT + P])
                last.then_inc(s_tp, 1)

            @block.vector
            def _(v):
                v.memset(ends[:, :], 0.0).then_inc(s_used, 1)
                v.memset(mat[:, :, :], 0.0)
                v.memset(pmap[:, :, 0:1], 1.0)
                v.memset(qmap[:, :, 0:1], 0.0)
                v.memset(wide[:, 0, STEPS:STEPS + 1], 1.0)
                v.memset(ops[:, :, STEPS:STEPS + 1], float(OUT))
                v.tensor_copy(spread[:, :, :], t.const[0:FIELDS, K_SPREAD:K_SPREAD + 4 * P].rearrange(
                    "p (k m) -> p k m", k=4)).then_inc(s_spread, 1)
                v.drain()
                for b in range(2):
                    last = v.tensor_copy(mat[:, b, b * P:(b + 1) * P], t.const[:, K_IDENT:K_IDENT + P])
                last.then_inc(s_mat, 1)
                n = v.value_load(t.n_sets[0:1, 0:1], min_val=1, max_val=max_sets)
                ri, rj, rcos, rsin = (ops[:, k, 0:STEPS] for k in range(4))
                kid = [t.const[:, K_ROW + b:K_ROW + b + 1] for b in range(2)]

                def next_end():
                    v.reduce_max(first[:, :], left[:, :], axis=mybir.AxisListType.X)
                    v.drain()
                    v.tensor_scalar(at[:, :], first[:, :], -1.0, float(STEPS + 1), ALU.mult, ALU.add)
                    v.scalar_tensor_tensor(left[:, 0:STEPS], left[:, 0:STEPS], first[:, 0:1], left[:, 0:STEPS],
                                           ALU.is_lt, ALU.mult)
                    v.drain()
                    k = v.value_load(at[0:1, 0:1], min_val=0, max_val=STEPS)
                    i_at, j_at, cos_at, sin_at = (ops[:, w, bass.ds(k, 1)] for w in range(4))
                    rows = t.const[:, K_ROW:K_ROW + 2]
                    for ij in range(2):
                        v.tensor_scalar(is_ij[:, ij, :], rows, (i_at, j_at)[ij], None, ALU.is_equal)
                    v.tensor_scalar(clamped[:, :].unsqueeze(2), ops[:, 0:2, bass.ds(k, 1)], float(D - 1), None,
                                    ALU.min)
                    v.tensor_copy(coming[:, 3, :].unsqueeze(2), pmap[:, :, bass.ds(k, 1)])
                    v.tensor_copy(coming[:, 4, :].unsqueeze(2), qmap[:, :, bass.ds(k, 1)])
                    v.drain()
                    for ij in range(2):
                        v.tensor_scalar(read[:, ij, :], rows, clamped[:, ij:ij + 1], None, ALU.is_equal)
                    v.scalar_tensor_tensor(only_i[:, :], is_ij[:, 1, :], 0.0, is_ij[:, 0, :],
                                           ALU.is_equal, ALU.mult)
                    v.tensor_scalar(part[:, 0, :], is_ij[:, 1, :], sin_at, None, ALU.mult)
                    v.drain()
                    v.tensor_scalar(part[:, 1, :], only_i[:, :], sin_at, None, ALU.mult)
                    v.tensor_tensor(written[:, :], only_i[:, :], is_ij[:, 1, :], ALU.add)
                    v.drain()
                    v.scalar_tensor_tensor(coming[:, 0, :], only_i[:, :], cos_at, part[:, 0, :], ALU.mult, ALU.add)
                    v.scalar_tensor_tensor(coming[:, 1, :], is_ij[:, 1, :], cos_at, part[:, 1, :], ALU.mult,
                                           ALU.subtract)
                    v.tensor_scalar(coming[:, 2, :], written[:, :], -1.0, 1.0, ALU.mult, ALU.add)
                    v.drain()

                with v.Fori(0, n) as s:
                    v.wait_ge(s_loaded, s + 1)
                    v.tensor_tensor(wide[:, 1, 0:STEPS], ri, rj, ALU.max)
                    v.tensor_scalar(wide[:, 2, 0:STEPS], ri, float(D - 1), None, ALU.is_equal)
                    v.drain()
                    v.tensor_scalar(wide[:, 1, 0:STEPS], wide[:, 1, 0:STEPS], float(D), None, ALU.is_lt)
                    v.scalar_tensor_tensor(wide[:, 2, 0:STEPS], rj, float(D - 1), wide[:, 2, 0:STEPS],
                                           ALU.is_equal, ALU.max)
                    for b in range(2):
                        v.tensor_scalar(hit[:, b, :], ri, kid[b], None, ALU.is_equal)
                    v.drain()
                    v.tensor_tensor(wide[:, 0, 0:STEPS], wide[:, 1, 0:STEPS], wide[:, 2, 0:STEPS], ALU.max)
                    for b in range(2):
                        v.scalar_tensor_tensor(signed[:, b, :], rj, kid[b], hit[:, b, :], ALU.is_equal, ALU.subtract)
                    v.drain()
                    v.tensor_scalar(plain[:, :], wide[:, 0, 0:STEPS], -1.0, 1.0, ALU.mult, ALU.add)
                    for b in range(2):
                        v.scalar_tensor_tensor(hit[:, b, :], rj, kid[b], hit[:, b, :], ALU.is_equal, ALU.add)
                    v.tensor_tensor(left[:, :], wide[:, 0, :], t.const[:, K_DOWN:K_DOWN + STEPS + 1], ALU.mult)
                    v.reduce_sum(ends[:, 1:2], wide[:, 0, :], axis=mybir.AxisListType.X)
                    v.drain()
                    v.tensor_tensor(trig[:, 0, :], rcos, plain[:, :], ALU.mult)
                    v.tensor_tensor(trig[:, 1, :], rsin, plain[:, :], ALU.mult)
                    v.tensor_tensor(ends[:, 1:2], ends[:, 1:2], ends[:, 0:1], ALU.add)
                    v.drain()
                    v.tensor_copy(ends_i[:, :], ends[:, :])
                    for b in range(2):
                        v.tensor_tensor(add[:, b, :], signed[:, b, :], trig[:, 1, :], ALU.mult)
                    for b in range(2):
                        v.scalar_tensor_tensor(coef[:, b, :], hit[:, b, :], 0.0, plain[:, :], ALU.is_equal, ALU.mult)
                        v.tensor_tensor(kept[:, b, :], hit[:, b, :], trig[:, 0, :], ALU.mult)
                    v.drain().then_inc(s_ends, 1)
                    for b in range(2):
                        v.tensor_tensor(coef[:, b, :], coef[:, b, :], kept[:, b, :], ALU.add)
                    v.tensor_copy(ends[:, 0:1], ends[:, 1:2])
                    v.drain()
                    for b in range(2):
                        v.tensor_tensor_scan(pmap[:, b, 1:STEPS + 1], coef[:, b, :], wide[:, 0, 0:STEPS], 1.0,
                                             ALU.mult, ALU.add)
                        v.tensor_tensor_scan(qmap[:, b, 1:STEPS + 1], coef[:, b, :], add[:, b, :], 0.0,
                                             ALU.mult, ALU.add)
                    v.drain()
                    g0 = v.value_load(ends_i[0:1, 0:1], min_val=0, max_val=t.pairs * PAIR + max_sets)
                    g1 = v.value_load(ends_i[0:1, 1:2], min_val=0, max_val=t.pairs * PAIR + max_sets)
                    next_end()
                    with v.Fori(g0, g1) as g:
                        v.tensor_copy(now[:, :, :], coming[:, :, :])
                        for ij in range(2):
                            for b in range(2):
                                v.tensor_scalar(pick[:, ij, b, :], t.const[:, K_ONES:K_ONES + P],
                                                read[:, ij, b:b + 1], None, ALU.mult)
                        v.drain()
                        for b in range(2):
                            v.tensor_scalar(rest[:, b, :], mat[:, b, :], now[:, 3, b:b + 1], None, ALU.mult)
                        v.drain()
                        v.wait_ge(s_255, g + 1)
                        for b in range(2):
                            v.scalar_tensor_tensor(mat[:, b, :], row255[:, 0:D], now[:, 4, b:b + 1],
                                                   rest[:, b, :], ALU.mult, ALU.add)
                        v.drain().then_inc(s_mapped, 1)
                        for b in range(2):
                            v.tensor_scalar(rest[:, b, :], mat[:, b, :], now[:, 2, b:b + 1], None, ALU.mult)
                        next_end()
                        v.wait_ge(s_ij, g + 1)
                        for ij in range(2):
                            for b in range(2):
                                v.scalar_tensor_tensor((rest, mat)[ij][:, b, :], rows_ij[:, ij, :],
                                                       now[:, ij, b:b + 1], rest[:, b, :], ALU.mult, ALU.add)
                            v.drain()
                        v.sem_inc(s_mat, 1)
                    v.drain().then_inc(s_used, 1)
                v.sem_inc(s_done, 1)
                v.wait_ge(s_tp, 1)
                v.tensor_copy(t.matT[:, :, :], tp[:, :, :])
                v.drain()


def mix_matrix(nc, t):
    with ExitStack() as ctx:
        mean = ctx.enter_context(nc.sbuf_tensor("mean", [P, 2], f32))
        tp = ctx.enter_context(nc.psum_tensor("tp", [P, 2, D], f32))
        s_mix = ctx.enter_context(nc.semaphore("s_mix"))
        s_tp = ctx.enter_context(nc.semaphore("s_tp"))
        with nc.Block() as block:
            @block.vector
            def _(v):
                for lb in range(2):
                    eye = t.const[:, K_PLANES + lb * D:K_PLANES + (lb + 1) * D]
                    v.tensor_tensor(t.mix[:, lb, 0:C], t.matT[:, lb, 0:C], eye[:, 0:C], ALU.add)
                    for x in range(3):
                        plane = slice(C * (1 + x), C * (2 + x))
                        v.tensor_tensor(t.mix[:, lb, plane], t.matT[:, lb, C + x:D:3], eye[:, plane], ALU.add)
                v.drain()
                v.reduce_sum(mean[:, :], t.mix[:, :, :], axis=mybir.AxisListType.X)
                v.drain()
                v.tensor_scalar(mean[:, :], mean[:, :], 1 / D, None, ALU.mult)
                v.drain()
                for lb in range(2):
                    v.tensor_scalar(t.mix[:, lb, :], t.mix[:, lb, :], mean[:, lb:lb + 1], None, ALU.subtract)\
                        .then_inc(s_mix, 1)
                v.drain()
                high_part(v, t.mix_high[:, :, :], t.mix[:, :, :])
                v.drain()
                v.tensor_tensor(t.mix_low[:, :, :], t.mix[:, :, :], t.mix_high[:, :, :], ALU.subtract)
                v.wait_ge(s_tp, 1)
                v.tensor_copy(t.mixT[:, :, :], tp[:, :, :])
                v.drain()

            @block.tensor
            def _(pe):
                pe.wait_ge(s_mix, 2)
                for cb in range(2):
                    for lb in range(2):
                        last = nc.tensor.transpose(tp[:, cb, lb * P:(lb + 1) * P],
                                                   t.mix[:, lb, cb * P:(cb + 1) * P],
                                                   t.const[:, K_IDENT:K_IDENT + P])
                last.then_inc(s_tp, 1)


def high_part(v, high, x):
    return v.tensor_copy(high, x)


def product_of_parts(nc, out, high, low, right_high, right_low, lb, i):
    left = [part[:, lb, i * P:(i + 1) * P] for part in (high, low)]
    right = [part[:, lb, :] for part in (right_high, right_low)]
    nc.tensor.matmul(out, left[0], right[1], start=lb == 0, stop=False)
    nc.tensor.matmul(out, left[0], right[0], start=False, stop=False)
    return nc.tensor.matmul(out, left[1], right[0], start=False, stop=lb == 1)


def node_stats(nc, d, t):
    n = t.chunks
    SLOTS = 4
    rows = d.h.rearrange("(c i p) f -> c p i f", i=TILES, p=P)
    with ExitStack() as ctx:
        def sb(name, shape, dt=f32):
            return ctx.enter_context(nc.sbuf_tensor(name, shape, dt))

        def ps(name, shape):
            return ctx.enter_context(nc.psum_tensor(name, shape, f32))

        def sem(name):
            return ctx.enter_context(nc.semaphore(name))

        xT = sb("xT", [P, SLOTS, 2, CHUNK])
        high = sb("high", [P, SLOTS, 2, CHUNK], f32r)
        low = sb("low", [P, SLOTS, 2, CHUNK], f32r)
        h = sb("h_sb", [P, SLOTS, TILES, 1 + D])
        squares = sb("squares", [P, TILES, D])
        ss = sb("ss", [P, SLOTS, TILES])
        std = sb("std", [P, SLOTS, TILES])
        var = sb("var", [P, SLOTS, TILES])
        inv = sb("inv", [P, SLOTS, TILES])
        near = sb("near", [P, SLOTS, TILES])
        corr = sb("corr", [P, SLOTS, TILES])
        y = ps("y", [P, 2, TILES, D])
        gram_a = ps("gram_a", [P, 512])
        gram_b = ps("gram_b", [P, 512])
        s_x = [sem(f"s_x{i}") for i in range(SLOTS)]
        s_hout = [sem(f"s_hout{i}") for i in range(SLOTS)]
        s_high, s_low, s_y, s_ss, s_std, s_r, s_h, s_gram, s_ones = map(
            sem, ("s_high", "s_low", "s_y", "s_ss", "s_std", "s_r", "s_h", "s_gram", "s_ones"))

        with nc.Block() as block:
            @block.sync
            def _(sp):
                for c in range(SLOTS):
                    sp.dma_start(xT[:, c], d.xT[c]).then_inc(s_x[c], 16)

                def turn(c, u, load=True):
                    if load:
                        sp.wait_ge(s_low, c + 1)
                        sp.dma_start(xT[:, u], d.xT[c + SLOTS]).then_inc(s_x[u], 16)
                    sp.wait_ge(s_h, c + 1)
                    sp.dma_start(rows[c], h[:, u, :, 1:1 + D]).then_inc(s_hout[u], 16)

                with sp.Fori(0, n // SLOTS - 1) as it:
                    for u in range(SLOTS):
                        turn(it * SLOTS + u, u)
                for c in range(n - SLOTS, n):
                    turn(c, c % SLOTS, load=False)
                for u in range(SLOTS):
                    sp.wait_ge(s_hout[u], n // SLOTS * 16)

            @block.tensor
            def _(pe):
                def products(c, u, warm=True):
                    pe.wait_ge(s_low, c + 1)
                    if warm:
                        pe.wait_ge(s_h, c - 1)
                    for i in range(TILES):
                        for lb in range(2):
                            last = product_of_parts(nc, y[:, u % 2, i, :], high[:, u], low[:, u],
                                                    t.mix_high, t.mix_low, lb, i)
                        last.then_inc(s_y, 1)

                def gram(c, u, start=False, stop=False):
                    pe.wait_ge(s_h, c + 1)
                    for i in range(TILES):
                        nc.tensor.matmul(gram_a[:, 0:1 + P], h[:, u, i, 1:1 + P], h[:, u, i, 0:1 + P],
                                         start=start and i == 0, stop=stop and i == TILES - 1)
                        last = nc.tensor.matmul(gram_b[:, 0:P], h[:, u, i, 1 + P:1 + D], h[:, u, i, 1 + P:1 + D],
                                                start=start and i == 0, stop=stop and i == TILES - 1)
                    last.then_inc(s_gram, 1)

                pe.wait_ge(s_ones, 1)
                for c in range(SLOTS):
                    products(c, c, c >= 2)
                    if c >= 2:
                        gram(c - 2, c - 2, start=c == 2)
                with pe.Fori(1, n // SLOTS) as it:
                    for u in range(SLOTS):
                        products(it * SLOTS + u, u)
                        gram(it * SLOTS + u - 2, (u - 2) % SLOTS)
                gram(n - 2, (n - 2) % SLOTS)
                gram(n - 1, (n - 1) % SLOTS, stop=True)

            @block.gpsimd
            def _(pool):
                def split(c, u):
                    pool.wait_ge(s_high, c + 1)
                    pool.tensor_tensor(low[:, u], xT[:, u], high[:, u], ALU.subtract).then_inc(s_low, 1)

                for c in range(SLOTS):
                    split(c, c)
                with pool.Fori(1, n // SLOTS) as it:
                    for u in range(SLOTS):
                        split(it * SLOTS + u, u)

            @block.scalar
            def _(act):
                def turn(c, u):
                    for i in range(TILES):
                        act.wait_ge(s_y, c * TILES + i // 2 * 2 + 2)
                        nc.scalar.activation(squares[:, i, :], y[:, u % 2, i, :], ACT.Square,
                                             accum_out=ss[:, u, i:i + 1]).then_inc(s_ss, 1)
                    act.wait_ge(s_ss, c * TILES + TILES)
                    nc.scalar.activation(std[:, u, :], ss[:, u, :], ACT.Sqrt, scale=1 / D, bias=t.eps[:, 0:1])\
                        .then_inc(s_std, 1)

                for c in range(SLOTS):
                    turn(c, c)
                with act.Fori(1, n // SLOTS) as it:
                    for u in range(SLOTS):
                        turn(it * SLOTS + u, u)

            @block.vector
            def _(v):
                v.memset(h[:, :, :, 0:1], 1.0).then_inc(s_ones, 1)
                AHEAD = 2

                def split(c, u, rnd, warm=True):
                    v.wait_ge(s_x[u], rnd * 16 + 16)
                    if warm:
                        v.wait_ge(s_y, (c - SLOTS + 1) * TILES)
                    high_part(v, high[:, u], xT[:, u]).then_inc(s_high, 1)

                def turn(c, u):
                    v.wait_ge(s_ss, c * TILES + TILES)
                    v.tensor_scalar(var[:, u, :], ss[:, u, :], 1 / D, EPS, ALU.mult, ALU.add).then_inc(s_r, 1)
                    v.wait_ge(s_std, c + 1)
                    v.reciprocal(inv[:, u, :], std[:, u, :]).then_inc(s_r, 1)
                    v.wait_ge(s_r, c * 5 + 2)
                    v.tensor_tensor(near[:, u, :], inv[:, u, :], var[:, u, :], ALU.mult).then_inc(s_r, 1)
                    v.wait_ge(s_r, c * 5 + 3)
                    v.scalar_tensor_tensor(corr[:, u, :], near[:, u, :], -0.5, inv[:, u, :], ALU.mult, ALU.mult)\
                        .then_inc(s_r, 1)
                    v.wait_ge(s_r, c * 5 + 4)
                    v.scalar_tensor_tensor(t.rstd1[:, bass.ds(c * TILES, TILES)], corr[:, u, :], 1.5, inv[:, u, :],
                                           ALU.add, ALU.mult).then_inc(s_r, 1)
                    v.wait_ge(s_r, c * 5 + 5)
                    for i in range(TILES):
                        last = v.tensor_scalar(h[:, u, i, 1:1 + D], y[:, u % 2, i, :],
                                               t.rstd1[:, bass.ds(c * TILES + i, 1)], None, ALU.mult)
                    last.then_inc(s_h, 1)

                def reused(c, u, rnd):
                    v.wait_ge(s_hout[u], rnd * 16)
                    v.wait_ge(s_gram, c - SLOTS + 1)
                    turn(c, u)

                for c in range(AHEAD):
                    split(c, c, 0, False)
                for c in range(SLOTS):
                    ahead = c + AHEAD
                    split(ahead, ahead % SLOTS, ahead // SLOTS, ahead >= SLOTS)
                    turn(c, c)
                with v.Fori(1, n // SLOTS - 1) as it:
                    for u in range(SLOTS):
                        ahead = u + AHEAD
                        split(it * SLOTS + ahead, ahead % SLOTS, it + ahead // SLOTS)
                        reused(it * SLOTS + u, u, it)
                for c in range(n - SLOTS, n):
                    if c + AHEAD < n:
                        split(c + AHEAD, (c + AHEAD) % SLOTS, (c + AHEAD) // SLOTS)
                    reused(c, c % SLOTS, c // SLOTS)
                v.wait_ge(s_gram, n)
                v.tensor_copy(t.gram[:, 0:1 + P], gram_a[:, 0:1 + P])
                v.tensor_copy(t.gram[:, 1 + P:1 + 2 * P], gram_b[:, 0:P])
                v.drain()


def edges(nc, d, t):
    n = t.pairs
    with ExitStack() as ctx:
        def sb(name, shape, dt=f32):
            return ctx.enter_context(nc.sbuf_tensor(name, shape, dt))

        def ps(name, shape):
            return ctx.enter_context(nc.psum_tensor(name, shape, f32))

        def sem(name):
            return ctx.enter_context(nc.semaphore(name))

        hs = sb("hs", [P, 2, 2, D])
        hd = sb("hd", [P, 2, 2, 1 + D])
        marked = sb("marked", [P, 2, 1 + D])
        rowd = sb("rowd", [P, 2, 1 + PAIR], i32)
        at_s = sb("at_s", [P, 2, 2], i32)
        at_d = sb("at_d", [P, 2, 2], i32)
        hsT = sb("hsT", [P, 2, 2, P])
        hdT = sb("hdT", [P, 2, 2, P])
        lhid = sb("lhid", [P, 2, P])
        tpw = sb("tpw", [P, 2, 4, C])
        dx = sb("dx", [P, 2, 3, C])
        dot = sb("dot", [P, 2, C])
        ma = sb("ma", [P, 2, C])
        mb = sb("mb", [P, 2, C])
        pp = sb("pp", [P, 2, C])
        mp = sb("mp", [P, 2, 3, C])
        mq = sb("mq", [P, 2, 3, C])
        msg = sb("msg", [P, 2, 2, 4, C])
        eq0 = sb("eq0", [P, 2, PAIR])
        own = sb("own", [P, 2, 2])
        eq1 = sb("eq1", [P, 2, P])
        ind = sb("ind", [P, 2, P])
        sumT = sb("sumT", [P, 2, 4, P])
        linT = sb("linT", [P, 4, P])
        sq = sb("sq", [P, 3, P])
        aff = sb("aff", [P, 2, P])
        vv = sb("vv", [P, P])
        pb = sb("pb", [P, P])
        pg = sb("pg", [P, P])
        basT = sb("basT", [P, 2, 4, P])
        o_sb = sb("o_sb", [P, 2, 2, D])
        sqo = sb("sqo", [P, 2, D])
        p_t = ps("p_t", [P, 2, 2, P])
        p_tpw = ps("p_tpw", [P, 2, 4, C])
        p_up = ps("p_up", [P, 2, 4, C])
        p_sum = ps("p_sum", [P, 4, P])
        p_lin = ps("p_lin", [P, 4, P])
        p_o = ps("p_o", [P, 2, D])
        p_carry = ps("p_carry", [P, 512])
        p_stat = ps("p_stat", [P, 512])

        s_hs = [sem(f"s_hs{i}") for i in range(2)]
        s_hd = [sem(f"s_hd{i}") for i in range(2)]
        s_row = [sem(f"s_row{i}") for i in range(2)]
        s_oout = [sem(f"s_oout{i}") for i in range(2)]
        s_hdout = [sem(f"s_hdout{i}") for i in range(2)]
        q = Named()
        (q.ths, q.hsT, q.thd, q.hdT, q.lhid, q.ptpw, q.tpw, q.up, q.m, q.mb, q.msg, q.gram, q.eq, q.own, q.ind, q.psum, q.carry, q.sum,
         q.plin, q.lin, q.bas, q.self, q.marked, q.o, q.osb, q.sq, q.stat, q.ats, q.atd, q.clear, q.go) = map(
            sem, ("s_ths", "s_hsT", "s_thd", "s_hdT", "s_lhid", "s_ptpw", "s_tpw", "s_up", "s_m", "s_mb", "s_msg",
                  "s_gram_recv", "s_eq", "s_own", "s_ind", "s_psum", "s_carry", "s_sum", "s_plin", "s_lin", "s_bas", "s_self", "s_marked", "s_o",
                  "s_osb", "s_sq", "s_stat", "s_ats", "s_atd", "s_clear", "s_go"))
        ident = t.const[:, K_IDENT:K_IDENT + P]
        UP, SELF, LIN, WB = 0, 2, 4, 6

        with nc.Block() as block:
            @block.sync
            def _(sp):
                def rows_in(p, u):
                    if before(p, 2):
                        sp.wait_ge(q.eq, p - 1)
                        sp.wait_ge(q.ind, p - 1)
                    sp.dma_start(rowd[:, u, :], d.dst_row[bass.ds(p * PAIR, 1 + PAIR)].partition_broadcast(P))\
                        .then_inc(s_row[u], 16)

                def hd_out(p, u):
                    sp.wait_ge(s_hd[u], of_slot(p, u, 32))
                    sp.dma_start(d.hd[p], hd[:, u, :, 1:1 + D]).then_inc(s_hdout[u], 16)

                def o_out(p, u):
                    sp.wait_ge(q.osb, p + 1)
                    sp.dma_start(d.o[p], o_sb[:, u]).then_inc(s_oout[u], 16)

                staged(sp, n, 2, [(0, rows_in), (3, hd_out), (5, o_out)])
                for u in range(2):
                    sp.wait_ge(s_oout[u], n // 2 * 16)
                    sp.wait_ge(s_hdout[u], n // 2 * 16)

            @block.gpsimd
            def _(pool):
                bound = pool.to_reg(t.chunks * CHUNK - 1)

                def senders(p, u):
                    if before(p, 2):
                        pool.wait_ge(q.ths, p - 1)
                    pool.tensor_copy(at_s[:, u, :], t.edge_idx[:, 0, bass.ds(p * 2, 2)]).then_inc(q.ats, 1)
                    pool.wait_ge(q.ats, p + 1)
                    pool.sem_inc(q.go, 1)
                    for j in range(2):
                        pool.indirect_dma_start(
                            hs[:, u, j, :], None, d.h, bass.IndirectOffsetOnAxis(ap=at_s[:, u, j:j + 1], axis=0),
                            bounds_check=bound, oob_is_err=False).then_inc(s_hs[u], 16)

                def receivers(p, u):
                    if before(p, 2):
                        pool.wait_ge(s_hdout[u], of_slot(p - 2, u))
                        pool.wait_ge(q.gram, p - 1)
                    pool.tensor_copy(at_d[:, u, :], t.edge_idx[:, 1, bass.ds(p * 2, 2)]).then_inc(q.atd, 1)
                    pool.wait_ge(q.atd, p + 1)
                    pool.sem_inc(q.go, 1)
                    for j in range(2):
                        pool.indirect_dma_start(
                            hd[:, u, j, 1:1 + D], None, d.h, bass.IndirectOffsetOnAxis(ap=at_d[:, u, j:j + 1], axis=0),
                            bounds_check=bound, oob_is_err=False).then_inc(s_hd[u], 16)

                def masks(p, u):
                    if before(p, 2):
                        pool.wait_ge(q.psum, p - 1)
                    pool.tensor_copy(own[:, u, :], t.dstf[:, bass.ds(p * 2, 2)]).then_inc(q.own, 1)
                    pool.wait_ge(q.own, p + 1)
                    pool.wait_ge(s_row[u], of_slot(p, u))
                    pool.sem_inc(q.go, 1)
                    pool.tensor_scalar(eq0[:, u, :], rowd[:, u, 1:1 + PAIR], own[:, u, 0:1], None, ALU.is_equal)
                    pool.tensor_scalar(eq1[:, u, :], rowd[:, u, 1 + P:1 + PAIR], own[:, u, 1:2], None, ALU.is_equal)\
                        .then_inc(q.eq, 1)

                staged(pool, n, 2, [(-1, senders), (1, masks), (2, receivers)])

            @block.tensor
            def _(pe):
                def senders_T(p, u):
                    pe.wait_ge(s_hs[u], of_slot(p, u, 32))
                    if before(p, 4):
                        pe.wait_ge(q.hdT, p - 3)
                    for j in range(2):
                        for b in range(2):
                            last = nc.tensor.transpose(p_t[:, j, b, :], hs[:, u, j, b * P:(b + 1) * P], ident)
                    last.then_inc(q.ths, 1)

                def sums(p, u):
                    pe.wait_ge(q.msg, p + 1)
                    pe.wait_ge(q.eq, p + 1)
                    if before(p):
                        pe.wait_ge(q.sum, p)
                    for j in range(2):
                        own = eq0[:, u, 0:P] if j == 0 else eq1[:, u, :]
                        for x in range(4):
                            last = nc.tensor.matmul(p_sum[j * C:(j + 1) * C, x, :], msg[:, u, j, x, :], own,
                                                    start=True, stop=j == 0)
                            if j == 1:
                                last = nc.tensor.matmul(p_sum[C:2 * C, x, :], msg[:, u, 0, x, :],
                                                        eq0[:, u, P:PAIR], start=False, stop=True)
                    last.then_inc(q.psum, 1)

                def receivers_T(p, u):
                    pe.wait_ge(s_hd[u], of_slot(p, u, 32))
                    pe.wait_ge(q.hsT, p + 4 if not isinstance(p, int) else min(p + 4, n))
                    for j in range(2):
                        for b in range(2):
                            last = nc.tensor.transpose(p_t[:, j, b, :], hd[:, u, j, 1 + b * P:1 + (b + 1) * P], ident)
                    last.then_inc(q.thd, 1)

                def up(p, u):
                    pe.wait_ge(q.hsT, p + 1)
                    if before(p):
                        pe.wait_ge(q.m, p)
                    for j in range(2):
                        for b in range(2):
                            last = nc.tensor.matmul(p_up[:, j, 2 * b:2 * b + 2, :], hsT[:, j, b, :],
                                                    t.bd[:, UP + b, :], start=True, stop=True)
                    last.then_inc(q.up, 1)

                def weights(p, u):
                    pe.wait_ge(q.lhid, p + 1)
                    if before(p):
                        pe.wait_ge(q.tpw, p)
                    for j in range(2):
                        last = nc.tensor.matmul(p_tpw[:, j, :, :], lhid[:, j, :],
                                                t.m4[:, :], start=True, stop=True)
                    last.then_inc(q.ptpw, 1)

                def lin(p, u):
                    pe.wait_ge(q.sum, p + 1)
                    if before(p):
                        pe.wait_ge(q.lin, p)
                    nc.tensor.matmul(p_lin[:, 0, :], t.bd[:, LIN, :], sumT[:, u, 0, :], start=True, stop=True)
                    nc.tensor.matmul(p_lin[:, 1:4, :], t.bd[:, LIN + 1, :], sumT[:, u, 1:4, :],
                                     start=True, stop=True).then_inc(q.plin, 1)
                    nc.tensor.matmul(p_carry[:, 0:4], t.const[:, K_DUP:K_DUP + P], sumT[:, u, :, P - 1],
                                     start=True, stop=True).then_inc(q.carry, 1)

                def self_part(p, u):
                    pe.wait_ge(q.hdT, p + 1)
                    if before(p):
                        pe.wait_ge(q.osb, p)
                    for j in range(2):
                        for b in range(2):
                            last = nc.tensor.matmul(p_o[:, j, b * P:(b + 1) * P], hdT[:, j, b, :],
                                                    t.bd[:, SELF + b, :], start=j == 0 and b == 0, stop=False,
                                                    skip_group_check=True)
                    last.then_inc(q.self, 1)

                def basis_part(p, u):
                    pe.wait_ge(q.bas, p + 1)
                    for x in range(4):
                        last = nc.tensor.matmul(p_o[:, :, x * C:(x + 1) * C], basT[:, u, x, :],
                                                t.bd[:, WB + min(x, 1), :], start=False, stop=x == 3,
                                                skip_group_check=True)
                    last.then_inc(q.o, 1)

                def gram(p, u):
                    pe.wait_ge(q.marked, p + 1)
                    for j in range(2):
                        first = isinstance(p, int) and p == 0 and j == 0
                        for left, right in ((slice(1, 1 + P), slice(0, 1 + P)), (slice(1 + P, 1 + D),) * 2):
                            last = nc.tensor.matmul(p_stat[:, right], hd[:, u, j, left], marked[:, j, right],
                                                    start=first and left.start == 1, stop=False,
                                                    skip_group_check=True)
                    last.then_inc(q.gram, 1)

                def stat(p, u):
                    pe.wait_ge(q.sq, p + 1)
                    for j in range(2):
                        for at, of in ((0, sqo[:, j, 0:C]), (1, sqo[:, j, C:2 * C]), (1, sqo[:, j, 2 * C:3 * C]),
                                       (1, sqo[:, j, 3 * C:D]), (2, o_sb[:, u, j, 0:C])):
                            last = nc.tensor.matmul(p_stat[0:1, D + 1 + at * C:D + 1 + (at + 1) * C],
                                                    marked[:, j, 0:1], of, start=False, stop=False,
                                                    skip_group_check=True)
                    last.then_inc(q.stat, 1)

                staged(pe, n, 2, [(1, up), (1, weights), (5, stat), (4, self_part), (0, senders_T), (2, sums), (3, lin),
                            (4, gram), (3, receivers_T), (4, basis_part)])

            @block.scalar
            def _(act):
                def hidden(p, u):
                    if before(p):
                        act.wait_ge(q.ptpw, p)
                    for j in range(2):
                        half = slice(j * C, (j + 1) * C)
                        last = nc.scalar.activation(lhid[half, j:j + 1, :], t.hidden[half, bass.ds(p, 1), :], ACT.Copy)
                    last.then_inc(q.lhid, 1)

                def senders_out(p, u):
                    act.wait_ge(q.ths, p + 1)
                    if before(p):
                        act.wait_ge(q.up, p)
                    nc.scalar.activation(hsT[:, :, :, :], p_t[:, :, :, :], ACT.Copy).then_inc(q.hsT, 1)

                def weights_out(p, u):
                    act.wait_ge(q.ptpw, p + 1)
                    if before(p):
                        act.wait_ge(q.mb, p)
                    for j in range(2):
                        nc.scalar.activation(tpw[:, j, 0:4:2, :], p_tpw[:, j, 0:4:2, :], ACT.Copy,
                                             scale=t.edge_sh0[:, bass.ds(p * 2 + j, 1)])
                    nc.scalar.activation(tpw[:, :, 1:4:2, :], p_tpw[:, :, 1:4:2, :], ACT.Copy).then_inc(q.tpw, 1)

                def receivers_out(p, u):
                    act.wait_ge(q.thd, p + 1)
                    if before(p):
                        act.wait_ge(q.self, p)
                    nc.scalar.activation(hdT[:, :, :, :], p_t[:, :, :, :], ACT.Copy).then_inc(q.hdT, 1)

                def lin_out(p, u):
                    act.wait_ge(q.plin, p + 1)
                    if before(p):
                        act.wait_ge(q.bas, p)
                    nc.scalar.activation(linT[:, :, :], p_lin[:, :, :], ACT.Copy)
                    nc.scalar.activation(sq[:, :, :], p_lin[:, 1:4, :], ACT.Square)
                    for k in range(2):
                        last = nc.scalar.activation(aff[:, k, :], p_lin[:, 0, :], ACT.Identity,
                                                    scale=t.wc[:, k:k + 1], bias=t.wc[:, 2 + k:3 + k])
                    last.then_inc(q.lin, 1)

                def mark(p, u):
                    act.wait_ge(s_hd[u], of_slot(p, u, 32))
                    if before(p):
                        act.wait_ge(q.stat, p)
                    for j in range(2):
                        last = nc.scalar.activation(marked[:, j, :], hd[:, u, j, :], ACT.Copy,
                                                    scale=t.last[:, bass.ds(p * 2 + j, 1)])
                    last.then_inc(q.marked, 1)

                def out_out(p, u):
                    act.wait_ge(q.o, p + 1)
                    if before(p, 2):
                        act.wait_ge(s_oout[u], of_slot(p - 2, u))
                    if before(p):
                        act.wait_ge(q.stat, p)
                    nc.scalar.activation(o_sb[:, u, :, :], p_o[:, :, :], ACT.Copy).then_inc(q.osb, 1)
                    act.wait_ge(q.osb, p + 1)
                    nc.scalar.activation(sqo[:, :, :], o_sb[:, u, :, :], ACT.Square).then_inc(q.sq, 1)

                act.wait_ge(q.clear, 1)
                staged(act, n, 2, [(1, weights_out), (0, hidden), (4, mark), (0, senders_out), (3, lin_out),
                             (3, receivers_out), (4, out_out)])

            @block.vector
            def _(v):
                def continued(p, u):
                    v.wait_ge(s_row[u], of_slot(p, u))
                    for j in range(2):
                        half = slice(j * C, (j + 1) * C)
                        last = v.tensor_scalar(ind[half, u, :], rowd[half, u, 1 + j * P:1 + (j + 1) * P],
                                               rowd[half, u, 0:1], None, ALU.is_equal)
                    last.then_inc(q.ind, 1)

                def message(p, u):
                    sh = t.edge_sh[:, bass.ds(p * 2, 2), :]
                    shx = sh[:, :, 1:4].unsqueeze(3).broadcast_to((P, 2, 3, C))
                    v.wait_ge(q.up, p + 1)
                    if before(p):
                        v.wait_ge(q.msg, p)
                    v.tensor_tensor(dx[:, :, :, :], p_up[:, :, 1:4, :], shx, ALU.mult)
                    v.wait_ge(q.tpw, p + 1)
                    v.tensor_tensor(pp[:, :, :], p_up[:, :, 0, :], tpw[:, :, 1, :], ALU.mult)
                    v.tensor_tensor(mq[:, :, :, :], p_up[:, :, 1:4, :],
                                    tpw[:, :, 2, :].unsqueeze(2).broadcast_to((P, 2, 3, C)), ALU.mult)
                    v.tensor_tensor(ma[:, :, :], p_up[:, :, 0, :], tpw[:, :, 0, :], ALU.mult).then_inc(q.m, 1)
                    v.drain()
                    v.tensor_tensor(dot[:, :, :], dx[:, :, 0, :], dx[:, :, 1, :], ALU.add)
                    v.tensor_tensor(mp[:, :, :, :], pp[:, :, :].unsqueeze(2).broadcast_to((P, 2, 3, C)), shx, ALU.mult)
                    v.drain()
                    v.tensor_tensor(dot[:, :, :], dot[:, :, :], dx[:, :, 2, :], ALU.add)
                    if before(p, 2):
                        v.wait_ge(q.psum, p - 1)
                    v.tensor_tensor(msg[:, u, :, 1:4, :], mp[:, :, :, :], mq[:, :, :, :], ALU.add)
                    v.drain()
                    v.tensor_tensor(mb[:, :, :], tpw[:, :, 3, :], dot[:, :, :], ALU.mult).then_inc(q.mb, 1)
                    v.drain()
                    v.tensor_tensor(msg[:, u, :, 0, :], ma[:, :, :], mb[:, :, :], ALU.add).then_inc(q.msg, 1)

                def carried(p, u):
                    v.wait_ge(q.psum, p + 1)
                    if before(p):
                        v.wait_ge(q.carry, p)
                        for x in range(4):
                            last = v.scalar_tensor_tensor(sumT[:, u, x, :], ind[:, u, :], p_carry[:, x:x + 1],
                                                          p_sum[:, x, :], ALU.mult, ALU.add)
                    else:
                        last = v.tensor_copy(sumT[:, u, :, :], p_sum[:, :, :])
                    last.then_inc(q.sum, 1)

                def basis(p, u):
                    A0, c4, w3, c0, w0, c2 = linT[:, 0, :], *(t.wc[:, k:k + 1] for k in (4, 5, 6, 7, 8))
                    v.wait_ge(q.lin, p + 1)
                    v.tensor_tensor(vv[:, :], sq[:, 0, :], sq[:, 1, :], ALU.add)
                    v.tensor_tensor(pb[:, :], aff[:, 0, :], A0, ALU.mult)
                    v.tensor_tensor(pg[:, :], aff[:, 1, :], A0, ALU.mult)
                    v.drain()
                    v.tensor_tensor(vv[:, :], vv[:, :], sq[:, 2, :], ALU.add)
                    v.drain()
                    v.scalar_tensor_tensor(pb[:, :], vv[:, :], c4, pb[:, :], ALU.mult, ALU.add)
                    v.scalar_tensor_tensor(pg[:, :], vv[:, :], w3, pg[:, :], ALU.mult, ALU.add)
                    v.drain()
                    v.scalar_tensor_tensor(pb[:, :], pb[:, :], c0, A0, ALU.add, ALU.mult)
                    if before(p, 2):
                        v.wait_ge(q.o, p - 1)
                    v.scalar_tensor_tensor(basT[:, u, 1:4, :], pg[:, :].unsqueeze(1).broadcast_to((P, 3, P)), w0,
                                           linT[:, 1:4, :], ALU.add, ALU.mult)
                    v.drain()
                    v.scalar_tensor_tensor(basT[:, u, 0, :], vv[:, :], c2, pb[:, :], ALU.mult, ALU.add)\
                        .then_inc(q.bas, 1)
                    v.drain()

                v.memset(hd[:, :, :, 0:1], 1.0)
                v.memset(lhid[:, :, :], 0.0).then_inc(q.clear, 1)
                staged(v, n, 2, [(1, continued), (1, message), (2, carried), (3, basis)])
                v.wait_ge(q.stat, n)
                v.tensor_tensor(t.gram[:, :], t.gram[:, :], p_stat[:, 0:1 + D], ALU.subtract)
                v.tensor_copy(t.edge_sums[:, :], p_stat[0:1, D + 1:D + 1 + 3 * C])
                v.drain()


def norms(nc, t):
    nodes = float(t.nodes)
    with ExitStack() as ctx:
        def sb(name, shape, dt=f32):
            return ctx.enter_context(nc.sbuf_tensor(name, shape, dt))

        gm = sb("gm", [P, 2, P])
        va = sb("va", [P, 3, C])
        r = sb("r", [P, 3, C])
        mom = sb("mom", [P, 2, C])
        std = sb("nstd", [P, 2, C])
        inv = sb("ninv", [P, 2, C])
        cor = sb("ncor", [P, 2, C])
        m1 = sb("nm1", [P, 1])
        fm = sb("fm", [P, 2, D])
        fmean = sb("fmean", [P, 2])
        ta = ctx.enter_context(nc.psum_tensor("ta", [P, 512], f32))
        rows = ctx.enter_context(nc.psum_tensor("rows", [P, 512], f32))
        pf = ctx.enter_context(nc.psum_tensor("pf", [P, 2, D], f32))
        s_g, s_t, s_v, s_rows, s_var, s_sd, s_f, s_pf = (
            ctx.enter_context(nc.semaphore(x)) for x in
            ("s_g", "s_t", "s_v", "s_rows", "s_var", "s_sd", "s_f", "s_pf"))
        low, high, ones = (t.const[:, k:k + P] for k in (K_LOW, K_HIGH, K_ONES))

        with nc.Block() as block:
            @block.vector
            def _(v):
                v.memset(gm[:, :, :], 0.0)
                v.drain()
                for b in range(2):
                    for j in range(2):
                        part = slice(j * C, (j + 1) * C)
                        at = 1 + b * P + j * C
                        last = v.tensor_copy(gm[part, b, part], t.gram[part, at:at + C])
                last = v.tensor_scalar(va[:, 2, :], t.wstk[:, 0, :], t.gram[:, 0:1], None, ALU.mult)
                last.then_inc(s_g, 1)
                v.wait_ge(s_t, 1)
                v.tensor_tensor(va[:, 0:2, :], t.wstk[:, :, :], ta[:, 0:2 * C].rearrange("p (b c) -> p b c", b=2),
                                ALU.mult).then_inc(s_v, 1)
                v.wait_ge(s_rows, 1)
                v.tensor_scalar(r[:, 0, :], rows[:, 0:C], 1 / nodes, None, ALU.mult)
                v.tensor_scalar(r[:, 1, :], rows[:, C:2 * C], 1 / (3 * nodes), EPS, ALU.mult, ALU.add)
                v.tensor_scalar(r[:, 2, :], rows[:, 2 * C:3 * C], 1 / nodes, None, ALU.mult)
                v.drain()
                v.tensor_tensor(mom[:, 0, :], r[:, 2, :], r[:, 2, :], ALU.mult)
                v.drain()
                v.tensor_tensor(mom[:, 0, :], r[:, 0, :], mom[:, 0, :], ALU.subtract)
                v.drain()
                v.tensor_scalar(r[:, 0, :], mom[:, 0, :], 0.0, EPS, ALU.max, ALU.add)
                v.drain().then_inc(s_var, 1)
                v.wait_ge(s_sd, 1)
                v.reciprocal(inv[:, :, :], std[:, :, :])
                v.drain()
                v.tensor_tensor(cor[:, :, :], inv[:, :, :], r[:, 0:2, :], ALU.mult)
                v.drain()
                v.scalar_tensor_tensor(cor[:, :, :], cor[:, :, :], -0.5, inv[:, :, :], ALU.mult, ALU.mult)
                v.drain()
                v.scalar_tensor_tensor(inv[:, :, :], cor[:, :, :], 1.5, inv[:, :, :], ALU.add, ALU.mult)
                v.drain()
                v.tensor_tensor(t.scale[:, 0:C], inv[:, 0, :], t.gb[:, 0, :], ALU.mult)
                for x in range(3):
                    v.tensor_tensor(t.scale[:, (1 + x) * C:(2 + x) * C], inv[:, 1, :], t.gb[:, 2, :], ALU.mult)
                v.memset(t.shift[:, :], 0.0)
                v.memset(fm[:, :, :], 0.0)
                v.drain()
                v.tensor_tensor(mom[:, 1, :], r[:, 2, :], t.scale[:, 0:C], ALU.mult)
                for b in range(2):
                    v.tensor_tensor(fm[:, b, b * P:(b + 1) * P], t.bd[:, 2 + b, :], t.scale[:, b * P:(b + 1) * P],
                                    ALU.mult)
                v.drain()
                v.tensor_tensor(t.shift[:, 0:C], t.gb[:, 1, :], mom[:, 1, :], ALU.subtract)
                for b in range(2):
                    v.tensor_tensor(fm[:, b, b * P:(b + 1) * P], fm[:, b, b * P:(b + 1) * P],
                                    t.const[:, K_IDENT:K_IDENT + P], ALU.add)
                v.drain()
                v.reduce_sum(m1[:, :], t.shift[:, 0:C], axis=mybir.AxisListType.X)
                v.reduce_sum(fmean[:, :], fm[:, :, :], axis=mybir.AxisListType.X)
                v.drain()
                v.tensor_scalar(m1[:, :], m1[:, :], 1 / D, None, ALU.mult)
                v.tensor_scalar(fmean[:, :], fmean[:, :], 1 / D, None, ALU.mult)
                v.drain()
                v.tensor_scalar(t.shift_c[:, :], t.shift[:, :], m1[:, 0:1], None, ALU.subtract)
                for b in range(2):
                    last = v.tensor_scalar(fm[:, b, :], fm[:, b, :], fmean[:, b:b + 1], None, ALU.subtract)
                v.drain().then_inc(s_f, 1)
                v.wait_ge(s_pf, 1)
                v.tensor_copy(t.fold[:, :, :], pf[:, :, :])
                v.drain()
                high_part(v, t.fold_high[:, :, :], t.fold[:, :, :])
                v.drain()
                v.tensor_tensor(t.fold_low[:, :, :], t.fold[:, :, :], t.fold_high[:, :, :], ALU.subtract)
                v.drain()

            @block.tensor
            def _(pe):
                pe.wait_ge(s_g, 1)
                for b in range(2):
                    last = nc.tensor.matmul(ta[:, b * C:(b + 1) * C], gm[:, b, :], t.wstk[:, b, :],
                                            start=True, stop=True)
                last.then_inc(s_t, 1)
                pe.wait_ge(s_v, 1)
                nc.tensor.matmul(rows[:, 0:3 * C], t.const[0:1, K_ONES:K_ONES + P], t.edge_sums[:, :],
                                 start=True, stop=False, skip_group_check=True)
                nc.tensor.matmul(rows[:, 0:C], low, va[:, 0, :], start=False, stop=False, skip_group_check=True)
                nc.tensor.matmul(rows[:, C:2 * C], high, va[:, 0, :], start=False, stop=False, skip_group_check=True)
                nc.tensor.matmul(rows[:, C:2 * C], ones, va[:, 1, :], start=False, stop=False, skip_group_check=True)
                nc.tensor.matmul(rows[:, 2 * C:3 * C], low, va[:, 2, :], start=False, stop=True,
                                 skip_group_check=True).then_inc(s_rows, 1)
                pe.wait_ge(s_f, 1)
                for lb in range(2):
                    for cb in range(2):
                        last = nc.tensor.matmul(pf[:, lb, :], t.mixT[:, cb, lb * P:(lb + 1) * P], fm[:, cb, :],
                                                start=cb == 0, stop=cb == 1)
                last.then_inc(s_pf, 1)

            @block.scalar
            def _(act):
                act.wait_ge(s_var, 1)
                nc.scalar.activation(std[:, :, :], r[:, 0:2, :], ACT.Sqrt).then_inc(s_sd, 1)


def node_outputs(nc, d, t):
    n = t.chunks
    SLOTS = 4
    rows = d.out.rearrange("(c i p) f -> c p i f", i=TILES, p=P)
    with ExitStack() as ctx:
        def sb(name, shape, dt=f32):
            return ctx.enter_context(nc.sbuf_tensor(name, shape, dt))

        def sem(name):
            return ctx.enter_context(nc.semaphore(name))

        xT = sb("xT2", [P, SLOTS, 2, CHUNK])
        high = sb("high2", [P, SLOTS, 2, CHUNK], f32r)
        low = sb("low2", [P, SLOTS, 2, CHUNK], f32r)
        z = sb("z", [P, SLOTS, TILES, D])
        res = sb("res", [P, SLOTS, TILES, D])
        squares = sb("squares2", [P, TILES, D])
        ss = sb("ss2", [P, SLOTS, TILES])
        less_half_var = sb("less_half_var", [P, SLOTS, TILES])
        std = sb("std2", [P, SLOTS, TILES])
        inv = sb("inv2", [P, SLOTS, TILES])
        near = sb("near2", [P, SLOTS, TILES])
        corr = sb("corr2", [P, SLOTS, TILES])
        rstd = sb("rstd2", [P, SLOTS, TILES])
        less_half_eps = sb("less_half_eps", [P, 1])
        zp = ctx.enter_context(nc.psum_tensor("zp", [P, SLOTS, TILES, D], f32))
        s_x = [sem(f"s2_x{i}") for i in range(SLOTS)]
        s_out = [sem(f"s2_out{i}") for i in range(SLOTS)]
        (s_high, s_low, s_zp, s_z, s_ss, s_std, s_inv, s_near, s_corr, s_rstd, s_res_v, s_res_act, s_eps) = map(
            sem, ("s2_high", "s2_low", "s2_zp", "s2_z", "s2_ss", "s2_std", "s2_inv", "s2_near", "s2_corr",
                  "s2_rstd", "s2_res_v", "s2_res_act", "s2_eps"))

        with nc.Block() as block:
            @block.sync
            def _(sp):
                def load(c, u):
                    if before(c, SLOTS):
                        sp.wait_ge(s_low, c - (SLOTS - 1))
                    sp.dma_start(xT[:, u], d.xT[c]).then_inc(s_x[u], 16)

                def store(c, u):
                    sp.wait_ge(s_res_v, c + 1)
                    sp.wait_ge(s_res_act, c + 1)
                    sp.dma_start(rows[c], res[:, u]).then_inc(s_out[u], 16)

                staged(sp, n, SLOTS, [(-4, load), (4, store)])
                for u in range(SLOTS):
                    sp.wait_ge(s_out[u], n // SLOTS * 16)

            @block.gpsimd
            def _(pool):
                def split(c, u):
                    pool.wait_ge(s_high, c + 1)
                    pool.tensor_tensor(low[:, u], xT[:, u], high[:, u], ALU.subtract).then_inc(s_low, 1)

                def newton(c, u):
                    pool.wait_ge(s_inv, c + 1)
                    pool.tensor_tensor(near[:, u, :], less_half_var[:, u, :], inv[:, u, :], ALU.mult)\
                        .then_inc(s_near, 1)
                    pool.wait_ge(s_near, c + 1)
                    pool.tensor_tensor(corr[:, u, :], near[:, u, :], inv[:, u, :], ALU.mult).then_inc(s_corr, 1)

                staged(pool, n, SLOTS, [(-1, split), (2, newton)])

            @block.tensor
            def _(pe):
                def products(c, u):
                    pe.wait_ge(s_low, c + 1)
                    if before(c, SLOTS):
                        pe.wait_ge(s_z, c - (SLOTS - 1))
                    for i in range(TILES):
                        for lb in range(2):
                            last = product_of_parts(nc, zp[:, u, i, :], high[:, u], low[:, u],
                                                    t.fold_high, t.fold_low, lb, i)
                    last.then_inc(s_zp, 1)

                staged(pe, n, SLOTS, [(0, products)])

            @block.scalar
            def _(act):
                def summed(c, u):
                    act.wait_ge(s_z, c + 1)
                    for i in range(TILES):
                        nc.scalar.activation(squares[:, i, :], z[:, u, i, :], ACT.Square,
                                             accum_out=ss[:, u, i:i + 1]).then_inc(s_ss, 1)
                    act.wait_ge(s_ss, c * TILES + TILES)
                    nc.scalar.activation(std[:, u, :], ss[:, u, :], ACT.Sqrt, scale=1 / D, bias=t.eps[:, 0:1])
                    nc.scalar.activation(less_half_var[:, u, :], ss[:, u, :], ACT.Identity, scale=-0.5 / D,
                                         bias=less_half_eps[:, 0:1]).then_inc(s_std, 1)

                def normed(c, u):
                    act.wait_ge(s_rstd, c + 1)
                    if before(c, SLOTS):
                        act.wait_ge(s_out[u], of_slot(c - SLOTS, u, 16, SLOTS))
                    for i in range(TILES // 2, TILES):
                        last = nc.scalar.activation(res[:, u, i, :], z[:, u, i, :], ACT.Copy, scale=rstd[:, u, i:i + 1])
                    last.then_inc(s_res_act, 1)

                act.wait_ge(s_eps, 1)
                staged(act, n, SLOTS, [(3, normed), (0, summed)])

            @block.vector
            def _(v):
                def split(c, u):
                    v.wait_ge(s_x[u], of_slot(c, u, 16, SLOTS))
                    if before(c, SLOTS):
                        v.wait_ge(s_zp, c - (SLOTS - 1))
                    high_part(v, high[:, u], xT[:, u]).then_inc(s_high, 1)

                def scaled(c, u):
                    v.wait_ge(s_zp, c + 1)
                    if before(c, SLOTS):
                        v.wait_ge(s_res_act, c - (SLOTS - 1))
                        v.wait_ge(s_res_v, c - (SLOTS - 1))
                    for i in range(TILES):
                        last = v.scalar_tensor_tensor(z[:, u, i, :], zp[:, u, i, :],
                                                      t.rstd1[:, bass.ds(c * TILES + i, 1)], t.shift_c[:, :],
                                                      ALU.mult, ALU.add)
                    last.then_inc(s_z, 1)

                def inverse(c, u):
                    v.wait_ge(s_std, c + 1)
                    v.reciprocal(inv[:, u, :], std[:, u, :]).then_inc(s_inv, 1)

                def normed(c, u):
                    v.wait_ge(s_corr, c + 1)
                    v.scalar_tensor_tensor(rstd[:, u, :], corr[:, u, :], 1.5, inv[:, u, :], ALU.add, ALU.mult)\
                        .then_inc(s_rstd, 1)
                    v.wait_ge(s_rstd, c + 1)
                    if before(c, SLOTS):
                        v.wait_ge(s_out[u], of_slot(c - SLOTS, u, 16, SLOTS))
                    for i in range(TILES // 2):
                        last = v.tensor_scalar(res[:, u, i, :], z[:, u, i, :], rstd[:, u, i:i + 1], None, ALU.mult)
                    last.then_inc(s_res_v, 1)

                v.memset(less_half_eps[:, :], -EPS / 2).then_inc(s_eps, 1)
                staged(v, n, SLOTS, [(-2, split), (0, scaled), (3, normed), (1, inverse)])


def receiver_outputs(nc, d, t):
    n = t.pairs
    SLOTS = 8
    with ExitStack() as ctx:
        def sb(name, shape, dt=f32):
            return ctx.enter_context(nc.sbuf_tensor(name, shape, dt))

        def sem(name):
            return ctx.enter_context(nc.semaphore(name))

        hd = sb("hd2", [P, SLOTS, 2, D])
        o = sb("o2", [P, SLOTS, 2, D])
        z = sb("z2", [P, SLOTS, 2, D])
        res = sb("res2", [P, SLOTS, 2, D])
        unused = sb("unused", [P, 2, 2, D])
        at = sb("at3", [P, SLOTS, 2], i32)
        total = sb("total", [P, SLOTS, 2])
        less_mean = sb("less_mean", [P, SLOTS, 2])
        ss = sb("ss3", [P, SLOTS, 2])
        std = sb("std3", [P, SLOTS, 2])
        inv = sb("inv3", [P, SLOTS, 2])
        s_in = [sem(f"s3_in{i}") for i in range(SLOTS)]
        s_put = [sem(f"s3_put{i}") for i in range(SLOTS)]
        s_read, s_z, s_total, s_mean, s_ss, s_std, s_inv, s_res, s_at, s_go = map(
            sem, ("s3_read", "s3_z", "s3_total", "s3_mean", "s3_ss", "s3_std", "s3_inv", "s3_res", "s3_at", "s3_go"))
        scale = t.scale[:, :].unsqueeze(1).broadcast_to((P, 2, D))
        shift = t.shift[:, 0:C].unsqueeze(1).broadcast_to((P, 2, C))

        with nc.Block() as block:
            @block.sync
            def _(sp):
                def load(p, u):
                    if before(p, SLOTS):
                        sp.wait_ge(s_read, p - (SLOTS - 1))
                    sp.dma_start(hd[:, u], d.hd[p]).then_inc(s_in[u], 16)
                    sp.dma_start(o[:, u], d.o[p]).then_inc(s_in[u], 16)

                staged(sp, n, SLOTS, [(0, load)])

            @block.gpsimd
            def _(pool):
                bound = pool.to_reg(t.chunks * CHUNK - 1)

                def put(p, u):
                    pool.wait_ge(s_res, p + 1)
                    pool.tensor_copy(at[:, u, :], t.put[:, bass.ds(p * 2, 2)]).then_inc(s_at, 1)
                    pool.wait_ge(s_at, p + 1)
                    pool.sem_inc(s_go, 1)
                    for j in range(2):
                        pool.indirect_dma_start(
                            d.out, bass.IndirectOffsetOnAxis(ap=at[:, u, j:j + 1], axis=0),
                            res[:, u, j, :], None, bounds_check=bound,
                            oob_is_err=False).then_inc(s_put[u], 16)

                staged(pool, n, SLOTS, [(0, put)])
                for u in range(SLOTS):
                    pool.wait_ge(s_put[u], (n + SLOTS - 1 - u) // SLOTS * 32)

            @block.scalar
            def _(act):
                def sums(p, u):
                    act.wait_ge(s_z, p + 1)
                    if before(p):
                        act.wait_ge(s_total, 2 * p)
                    for j in range(2):
                        nc.scalar.activation(unused[:, 0, j, :], z[:, u, j, :], ACT.Copy,
                                             accum_out=total[:, u, j:j + 1]).then_inc(s_total, 1)

                def squares(p, u):
                    act.wait_ge(s_mean, p + 1)
                    if before(p):
                        act.wait_ge(s_ss, 2 * p)
                    for j in range(2):
                        nc.scalar.activation(unused[:, 1, j, :], z[:, u, j, :], ACT.Square,
                                             bias=less_mean[:, u, j:j + 1],
                                             accum_out=ss[:, u, j:j + 1]).then_inc(s_ss, 1)

                def root(p, u):
                    act.wait_ge(s_ss, 2 * p + 2)
                    nc.scalar.activation(std[:, u, :], ss[:, u, :], ACT.Sqrt, scale=1 / D, bias=t.eps[:, 0:1])\
                        .then_inc(s_std, 1)

                staged(act, n, SLOTS, [(3, root), (1, sums), (2, squares)])

            @block.vector
            def _(v):
                def summed(p, u):
                    v.wait_ge(s_in[u], of_slot(p, u, 32, SLOTS))
                    v.tensor_tensor(z[:, u], o[:, u], scale, ALU.mult)
                    v.drain()
                    v.tensor_tensor(z[:, u], z[:, u], hd[:, u], ALU.add).then_inc(s_read, 1)

                def shifted(p, u):
                    v.wait_ge(s_read, p + 1)
                    v.tensor_tensor(z[:, u, :, 0:C], z[:, u, :, 0:C], shift, ALU.add).then_inc(s_z, 1)

                def mean(p, u):
                    v.wait_ge(s_total, 2 * p + 2)
                    v.tensor_scalar(less_mean[:, u, :], total[:, u, :], -1 / D, None, ALU.mult).then_inc(s_mean, 1)

                def inverse(p, u):
                    v.wait_ge(s_std, p + 1)
                    v.reciprocal(inv[:, u, :], std[:, u, :]).then_inc(s_inv, 1)

                def normed(p, u):
                    if before(p, SLOTS):
                        v.wait_ge(s_put[u], of_slot(p - SLOTS, u, 32, SLOTS))
                    v.wait_ge(s_inv, p + 1)
                    for j in range(2):
                        last = v.tensor_scalar(res[:, u, j, :], z[:, u, j, :], less_mean[:, u, j:j + 1],
                                               inv[:, u, j:j + 1], ALU.add, ALU.mult)
                    last.then_inc(s_res, 1)

                staged(v, n, SLOTS, [(2, mean), (4, inverse), (0, summed), (4, normed), (0, shifted)])


def build(nc, d, shapes, phases=None):
    with ExitStack() as ctx:
        t = tensors(nc, ctx, shapes)
        with nc.sbuf_tensor("packed", [FIELDS, t.pairs * PAIR + 2 * P], bf16) as packed:
            prepare(nc, d, t, packed)
            rotate(nc, t, packed)
        mix_matrix(nc, t)
        node_stats(nc, d, t)
        edges(nc, d, t)
        norms(nc, t)
        node_outputs(nc, d, t)
        receiver_outputs(nc, d, t)


def arrays_of(inputs):
    x = np.asarray(inputs["x"])
    src, dst = np.asarray(inputs["src"]), np.asarray(inputs["dst"])
    nodes, n_edges = x.shape[0], src.shape[0]
    chunks = -(-(nodes + 1) // (CHUNK * 4)) * 4
    pairs = -(-n_edges // (PAIR * 2)) * 2
    e = pairs * PAIR
    xp = np.zeros((chunks * CHUNK, D), np.float32)
    xp[:nodes] = x
    srcp, dstp = np.full(e, nodes, np.int32), np.full(e, nodes, np.int32)
    srcp[:n_edges], dstp[:n_edges] = src, dst
    nxt = np.full(e, nodes + 1, np.int32)
    nxt[:-1] = dstp[1:]
    row = np.full(e + 1, nodes + 1, np.int32)
    row[1:] = dstp
    angle = np.zeros(e, np.float32)
    angle[:n_edges] = np.asarray(inputs["edge_weight"])
    rbf = np.zeros((e, 16), np.float32)
    rbf[:n_edges] = np.asarray(inputs["edge_attr_16"])
    sh = np.zeros((e, 4), np.float32)
    sh[:n_edges] = np.asarray(inputs["edge_attr_4"])
    cols = lambda a: a.reshape((2 * pairs, P) + a.shape[1:]).swapaxes(0, 1)
    w = {k[len("L1_gnn_"):]: np.asarray(v) for k, v in inputs.items() if k.startswith("L1_gnn_")}

    def blocks(a, b):
        out = np.zeros((a.shape[0] + b.shape[0], a.shape[1] + b.shape[1]), np.float32)
        out[:a.shape[0], :a.shape[1]] = a
        out[a.shape[0]:, a.shape[1]:] = b
        return out

    bd = np.stack([blocks(w["W_up0"], w["W_up1"]), blocks(w["W_up1"], w["W_up1"]),
                   blocks(w["Wsc0"], w["Wsc1"]), blocks(w["Wsc1"], w["Wsc1"]),
                   blocks(w["W_lin0"], w["W_lin0"]), blocks(w["W_lin1"], w["W_lin1"]),
                   blocks(w["WB0"], w["WB0"]), blocks(w["WB1"], w["WB1"])], 1)
    twice = lambda a: np.concatenate([a, a], 0)
    c, g = w["Wc0"], w["Wc1"]
    wc = twice(np.stack([c[:, 3], g[:, 2], c[:, 1], g[:, 1], c[:, 4], g[:, 3], c[:, 0], g[:, 0], c[:, 2]], 1))
    k = np.zeros((P, K_ALL), np.float32)
    part, low = np.arange(P), np.arange(P) < C
    k[:, K_IDENT:K_IDENT + P] = np.eye(P)
    k[:, K_DUP:K_DUP + P] = (part[:, None] == C + part[None, :] % C)
    k[:, K_LOW:K_LOW + P] = low[:, None]
    k[:, K_HIGH:K_HIGH + P] = ~low[:, None]
    k[:, K_ONES:K_ONES + P] = 1
    k[:, K_TRI:K_TRI + P] = part[:, None] < part[None, :]
    source = np.concatenate([np.arange(C)] + [C + 3 * np.arange(C) + a for a in range(3)])
    for lb in range(2):
        k[:, K_PLANES + lb * D:K_PLANES + (lb + 1) * D] = (lb * P + part)[:, None] == source[None, :]
    k[P - 1, K_ROW127:K_ROW127 + P] = 1
    k[:, K_ROW:K_ROW + 2] = part[:, None] + P * np.arange(2)
    k[:, K_IOTA:K_IOTA + 2 * P] = np.arange(2 * P)
    for field, value in enumerate((0, 1, 2, 2, 2, 3, 3, 3)):
        k[field, K_SPREAD + value * P:K_SPREAD + (value + 1) * P] = 1
    k[:, K_DOWN:K_DOWN + STEPS + 1] = STEPS + 1 - np.arange(STEPS + 1)
    arrays = {
        "xT": xp.reshape(chunks, CHUNK, 2, P).transpose(0, 3, 2, 1),
        "steps": np.stack([cols(srcp), cols(dstp), cols(angle.view(np.int32))], 1),
        "rbf": rbf.reshape(pairs // 2, 2, 2, P, 16).transpose(0, 2, 4, 1, 3).reshape(pairs // 2, 32, 2 * P),
        "edge_idx": np.stack([cols(srcp), cols(dstp), cols(nxt)], 1),
        "edge_sh": cols(sh),
        "dst_row": row,
        "const": k,
        "bd": bd,
        "m1": blocks(w["M1"], w["M1"]),
        "m23": np.stack([blocks(w["M2"], w["M2"]), blocks(w["M3"], w["M3"])], 1),
        "m4": twice(w["M4"]),
        "wstk": np.stack([np.concatenate([w["Wsc0"], w["Wsc1"]], 0), twice(w["Wsc1"])], 1),
        "wc": wc,
        "gb": np.stack([w["gamma0"], w["beta0"], w["gamma1"]], 0),
    }
    arrays = {n: np.ascontiguousarray(a) for n, a in arrays.items()}
    return arrays, {"nodes": nodes, "chunks": chunks, "pairs": pairs}


def declare(nc, arrays, shapes):
    def given(name):
        a = arrays[name]
        return nc.dram_tensor(f"in_{name}", a.shape, mybir.dt.from_np(a.dtype), kind="ExternalInput").ap()

    d = Named()
    d.xT, d.steps, d.rbf, d.const = given("xT"), given("steps"), given("rbf"), given("const")
    d.edge_idx, d.edge_sh, d.dst_row = given("edge_idx"), given("edge_sh"), given("dst_row")
    d.bd, d.m1, d.m23, d.m4 = given("bd"), given("m1"), given("m23"), given("m4")
    d.wstk, d.wc, d.gb = given("wstk"), given("wc"), given("gb")
    n = shapes["chunks"] * CHUNK
    d.out = nc.dram_tensor("out", (n, D), f32, kind="ExternalOutput").ap()
    d.h = nc.dram_tensor("h_scratch", (n, D), f32, kind="Internal").ap()
    d.hd = nc.dram_tensor("hd_scratch", (shapes["pairs"], P, 2, D), f32, kind="Internal").ap()
    d.o = nc.dram_tensor("o_scratch", (shapes["pairs"], P, 2, D), f32, kind="Internal").ap()
    return d


def kernel(**inputs):
    import concourse.bacc as bacc
    from concourse.bass_utils import run_bass_kernel_spmd

    arrays, shapes = arrays_of(inputs)
    nc = bacc.Bacc("TRN2", target_bir_lowering=False, num_devices=1)
    d = declare(nc, arrays, shapes)
    build(nc, d, shapes)
    got = run_bass_kernel_spmd(nc, [{f"in_{n}": a for n, a in arrays.items()}], core_ids=[0])
    planes = got.results[0]["out"][:shapes["nodes"]].reshape(-1, 4, C)
    return np.concatenate([planes[:, 0], planes[:, 1:].swapaxes(1, 2).reshape(-1, 3 * C)], 1)
```
